# Optimizing a Trainium2 kernel written in Bass

```python
import numpy as np
import jax
import jax.numpy as jnp

def _softmax(x, axis=-1):
    return jax.nn.softmax(x, axis=axis)

def _gelu(x):
    return jax.nn.gelu(x, approximate=True)

def _silu(x):
    return jax.nn.silu(x)

def _sigmoid(x):
    return jax.nn.sigmoid(x)

def _layernorm(x, axis=-1, eps=1e-05):
    m = jnp.mean(x, axis=axis, keepdims=True)
    v = jnp.var(x, axis=axis, keepdims=True)
    return (x - m) / jnp.sqrt(v + eps)

def _scatter_add(tgt, idx, src, axis=0):
    return tgt.at[idx].add(src)

def _segment_sum(src, seg, n):
    return jax.ops.segment_sum(src, seg, n)
kernel_name = 'mk_prb_d1_jaxref_r2_a3d7d2'

def setup_inputs(seed: int=0):
    np.random.seed(seed)
    _w = jnp.asarray

    def _L0_attn_setup():
        import jax, jax.numpy as jnp
        import numpy as np
        import math
        NUM_HEADS = 16
        WINDOW = 128
        EPS = 1e-06

        def _telephone_block(x, g, Wqkv, Wo):
            B, S, D = x.shape
            H, dh, W = (NUM_HEADS, D // NUM_HEADS, WINDOW)
            nb = S // W
            xn = x * jax.lax.rsqrt(jnp.mean(x * x, axis=-1, keepdims=True) + EPS) * g
            qkv = xn @ Wqkv
            q, k, v = jnp.split(qkv, 3, axis=-1)

            def split_heads(t):
                return t.reshape(B, nb, W, H, dh).transpose(0, 3, 1, 2, 4)
            q, k, v = (split_heads(q), split_heads(k), split_heads(v))

            def shift_prev(t):
                return jnp.pad(t[:, :, :-1], ((0, 0), (0, 0), (1, 0), (0, 0), (0, 0)))
            k_ext = jnp.concatenate([shift_prev(k), k], axis=3)
            v_ext = jnp.concatenate([shift_prev(v), v], axis=3)
            scale = 1.0 / math.sqrt(dh)
            scores = jnp.einsum('bhnqd,bhnkd->bhnqk', q, k_ext) * scale
            i = jnp.arange(W)[:, None]
            j = jnp.arange(2 * W)[None, :]
            base = (j > i) & (j <= i + W)
            first = base & (j >= W)
            blk0 = (jnp.arange(nb) == 0)[:, None, None]
            mask = jnp.where(blk0, first[None], base[None])
            scores = jnp.where(mask[None, None], scores, jnp.finfo(scores.dtype).min)
            p = jax.nn.softmax(scores, axis=-1)
            o = jnp.einsum('bhnqk,bhnkd->bhnqd', p, v_ext)
            o = o.transpose(0, 2, 3, 1, 4).reshape(B, S, D)
            h = o @ Wo
            return x + h
        key = jax.random.key(seed)
        k1, k2, k3, k4 = jax.random.split(key, 4)
        B, S, D = (4, 2048, 512)
        x = jax.random.normal(k1, (B, S, D), dtype=jnp.float32)
        g = jnp.ones((D,), dtype=jnp.float32)
        Wqkv = jax.random.normal(k2, (D, 3 * D), dtype=jnp.float32) * 0.02
        Wo = jax.random.normal(k3, (D, D), dtype=jnp.float32) * 0.02
        return {'x': x, 'g': g, 'Wqkv': Wqkv, 'Wo': Wo}
    _L0_attn_in = _L0_attn_setup()

    def _L0_ffn_setup():
        import jax, jax.numpy as jnp
        import numpy as np
        E = 128
        D = 512
        C = 128
        key = jax.random.key(seed)
        kx, kg, ke = jax.random.split(key, 3)
        x = jax.random.normal(kx, (4, 1024, D), dtype=jnp.float32)
        wg = jax.random.normal(kg, (D, E), dtype=jnp.float32) * 0.02
        we = jax.random.normal(ke, (E, D, D), dtype=jnp.float32) * 0.02
        return {'x': x, 'wg': wg, 'we': we}
    _L0_ffn_in = _L0_ffn_setup()
    _d = {'L0_attn_x': _L0_attn_in['x'], 'L0_attn_g': _L0_attn_in['g'], 'L0_attn_Wqkv': _L0_attn_in['Wqkv'], 'L0_attn_Wo': _L0_attn_in['Wo'], 'L0_ffn_wg': _L0_ffn_in['wg'], 'L0_ffn_we': _L0_ffn_in['we']}
    _x0 = _d['L0_attn_x']
    _d['L0_attn_x'] = jax.random.normal(jax.random.fold_in(jax.random.key(seed), 1), (4, 2048, 512), dtype=_x0.dtype)
    del _x0
    return _d

def reference(L0_attn_x, L0_attn_g, L0_attn_Wqkv, L0_attn_Wo, L0_ffn_wg, L0_ffn_we):

    def _L0_attn_ref(x, g, Wqkv, Wo):
        import jax, jax.numpy as jnp
        import numpy as np
        import math
        NUM_HEADS = 16
        WINDOW = 128
        EPS = 1e-06

        def _telephone_block(x, g, Wqkv, Wo):
            B, S, D = x.shape
            H, dh, W = (NUM_HEADS, D // NUM_HEADS, WINDOW)
            nb = S // W
            xn = x * jax.lax.rsqrt(jnp.mean(x * x, axis=-1, keepdims=True) + EPS) * g
            qkv = xn @ Wqkv
            q, k, v = jnp.split(qkv, 3, axis=-1)

            def split_heads(t):
                return t.reshape(B, nb, W, H, dh).transpose(0, 3, 1, 2, 4)
            q, k, v = (split_heads(q), split_heads(k), split_heads(v))

            def shift_prev(t):
                return jnp.pad(t[:, :, :-1], ((0, 0), (0, 0), (1, 0), (0, 0), (0, 0)))
            k_ext = jnp.concatenate([shift_prev(k), k], axis=3)
            v_ext = jnp.concatenate([shift_prev(v), v], axis=3)
            scale = 1.0 / math.sqrt(dh)
            scores = jnp.einsum('bhnqd,bhnkd->bhnqk', q, k_ext) * scale
            i = jnp.arange(W)[:, None]
            j = jnp.arange(2 * W)[None, :]
            base = (j > i) & (j <= i + W)
            first = base & (j >= W)
            blk0 = (jnp.arange(nb) == 0)[:, None, None]
            mask = jnp.where(blk0, first[None], base[None])
            scores = jnp.where(mask[None, None], scores, jnp.finfo(scores.dtype).min)
            p = jax.nn.softmax(scores, axis=-1)
            o = jnp.einsum('bhnqk,bhnkd->bhnqd', p, v_ext)
            o = o.transpose(0, 2, 3, 1, 4).reshape(B, S, D)
            h = o @ Wo
            return x + h
        return _telephone_block(x, g, Wqkv, Wo)

    def _L0_ffn_ref(x, wg, we):
        import jax, jax.numpy as jnp
        import numpy as np
        E = 128
        D = 512
        C = 128
        B, S, d = x.shape
        xt = x.reshape(-1, d)
        T = xt.shape[0]
        logits = xt @ wg
        gates = jax.nn.softmax(logits, axis=-1)
        e1 = jnp.argmax(gates, axis=-1)
        mask1 = jax.nn.one_hot(e1, E, dtype=logits.dtype)
        logits2 = jnp.where(mask1 > 0, -jnp.inf, logits)
        e2 = jnp.argmax(logits2, axis=-1)
        mask2 = jax.nn.one_hot(e2, E, dtype=logits.dtype)
        g1 = jnp.take_along_axis(gates, e1[:, None], 1)[:, 0]
        g2 = jnp.take_along_axis(gates, e2[:, None], 1)[:, 0]
        denom = jnp.maximum(g1 + g2, jnp.finfo(gates.dtype).eps)
        g1, g2 = (g1 / denom, g2 / denom)
        loc1 = jnp.take_along_axis(jnp.cumsum(mask1, axis=0), e1[:, None], 1)[:, 0].astype(jnp.int32) - 1
        counts1 = mask1.sum(axis=0)
        loc2 = (jnp.take_along_axis(jnp.cumsum(mask2, axis=0), e2[:, None], 1)[:, 0] + counts1[e2]).astype(jnp.int32) - 1
        v1 = (loc1 < C).astype(xt.dtype)
        v2 = (loc2 < C).astype(xt.dtype)
        idx1 = e1.astype(jnp.int32) * C + jnp.minimum(loc1, C - 1)
        idx2 = e2.astype(jnp.int32) * C + jnp.minimum(loc2, C - 1)
        buf = jnp.zeros((E * C, d), dtype=xt.dtype)
        buf = buf.at[idx1].add(xt * v1[:, None])
        buf = buf.at[idx2].add(xt * v2[:, None])
        yb = jnp.einsum('ecd,edf->ecf', buf.reshape(E, C, d), we).reshape(E * C, d)
        y = (g1 * v1)[:, None] * yb[idx1] + (g2 * v2)[:, None] * yb[idx2]
        return y.reshape(B, S, d)
    x = L0_attn_x
    xn = _layernorm(x, axis=-1)
    x = x + _L0_attn_ref(xn, L0_attn_g, L0_attn_Wqkv, L0_attn_Wo) + _L0_ffn_ref(xn, L0_ffn_wg, L0_ffn_we)
    return x

_drawn_inputs = setup_inputs


def setup_inputs(seed=0):
    import zlib

    import numpy as np

    out = dict(_drawn_inputs(seed))
    spreads = {'L0_attn_g': (1.0, 0.6)}
    factors = {'L0_attn_Wqkv': 5.299, 'L0_attn_Wo': 5.261}
    for name, (base, spread) in spreads.items():
        noise = np.random.default_rng([zlib.crc32(name.encode()), seed]).standard_normal(out[name].shape)
        drawn = base * np.exp(spread * noise) if base else spread * noise
        out[name] = jnp.asarray(drawn.astype(out[name].dtype))
    for name, factor in factors.items():
        out[name] = (out[name] * factor).astype(out[name].dtype)
    return out
```

```python
from contextlib import ExitStack

import concourse.bass as bass
from concourse import mybir

F32 = mybir.dt.float32
F32R = mybir.dt.float32r
BF16 = mybir.dt.bfloat16
I32 = mybir.dt.int32
U32 = mybir.dt.uint32
I8 = mybir.dt.int8
ALU = mybir.AluOpType
ACT = mybir.ActivationFunctionType
AX = mybir.AxisListType

P = 128
NUM_HEADS = 16
LN_EPS = 1e-5
RMS_EPS = 1e-6
GATE_EPS = 1.1920929e-07
MASKED = -3.0e38


def wait(eng, sem, value):
    if isinstance(value, int) and value <= 0:
        return
    eng.wait_ge(sem, value)


class Chain:

    def __init__(self, eng, sem, base):
        self.eng, self.sem, self.base, self.n = eng, sem, base, 0

    def did(self, ins):
        ins.then_inc(self.sem, 1)
        self.n += 1

    def settle(self):
        self.eng.wait_ge(self.sem, self.base + self.n)


def repeated(eng, count, body):
    body(0)
    with eng.Fori(1, count - 1) as i:
        body(i)
    body(count - 1)


def is_last(i, count):
    return isinstance(i, int) and i == count - 1


def is_first(i):
    return isinstance(i, int) and i == 0


def telephone_moe(nc, x, g, wqkv, wo, wg, we, out):
    B, S, D = x.shape
    T = B * S
    E = wg.shape[1]
    CAP = P
    KT = D // P
    H, DH = NUM_HEADS, D // NUM_HEADS
    SCALE = float(DH) ** -0.5
    NT = T // P
    TB = 4
    NB = NT // TB
    EB = 4
    NE = E // EB
    NP = NT // 2
    GRP = H // 4
    PER_SEQ = S // P // TB
    assert D == 512 and E == 128 and DH == 32 and CAP == 128

    x_rows = x.rearrange("b s d -> (b s) d")
    out_rows = out.rearrange("b s d -> (b s) d")
    xa_rows = nc.dram_tensor("xa_rows", [T, D], F32, kind="Internal")
    xpx_rows = nc.dram_tensor("xpx_rows", [T, D], F32, kind="Internal")
    yb_rows = nc.dram_tensor("yb_rows", [E * CAP, D], F32, kind="Internal")

    ctx = ExitStack()
    early = ExitStack()
    with ctx:
        def sb(name, shape, dt=F32, where=ctx):
            return where.enter_context(nc.sbuf_tensor(name, shape, dt))

        def sem(name):
            return ctx.enter_context(nc.semaphore(name))

        def sems(name, n):
            return [sem(f"{name}{k}") for k in range(n)]

        wqkv_hi = sb("wqkv_hi", [P, KT, 3 * D], F32R)
        wqkv_lo = sb("wqkv_lo", [P, KT, 3 * D], F32R)
        wo_hi = sb("wo_hi", [P, KT, D], F32R)
        wo_lo = sb("wo_lo", [P, KT, D], F32R)
        ident = sb("ident", [P, P])
        above = sb("above", [P, 4, P], I8)
        keep_cur = sb("keep_cur", [P, 4 * P], BF16)
        keep_prev = sb("keep_prev", [P, 4 * P], BF16)
        prev_cap = sb("prev_cap", [P, NB])
        slot1 = sb("slot1", [P, NT], I32)
        slot2 = sb("slot2", [P, NT], I32)
        w1 = sb("w1", [P, NT])
        w2 = sb("w2", [P, NT])

        def early_sb(name, shape, dt=F32):
            return sb(name, shape, dt, early)

        tri = early_sb("tri", [P, P], BF16)
        ones = early_sb("ones", [P, P], BF16)
        zeros = early_sb("zeros", [P, 2 * P], BF16)
        iota_row = early_sb("iota_row", [P, P])
        tile_no = early_sb("tile_no", [P, NT])
        lane = early_sb("lane", [P, 1])
        gvec = early_sb("gvec", [P, KT])
        wgate = early_sb("wgate", [P, KT, E])
        raw = early_sb("raw", [P, 2, KT * D])
        x1 = early_sb("x1", [P, TB, D])
        xa1 = early_sb("xa1", [P, TB, D])
        xp1 = early_sb("xp1", [P, TB, D])
        xT1 = early_sb("xT1", [P, 2, KT, P])
        bn6 = early_sb("bn6", [P, TB, 6])
        mv = early_sb("mv", [P, TB, 2])
        ve = early_sb("ve", [P, TB])
        root = early_sb("root", [P, TB])
        rstd = early_sb("rstd", [P, TB])
        r2 = early_sb("r2", [P, TB])
        tmp4 = early_sb("tmp4", [P, TB])
        ms = early_sb("ms", [P, TB])
        comb = early_sb("comb", [P, TB])
        ir2 = early_sb("ir2", [P, NT])
        logit_all = early_sb("logit_all", [P, NT, E])
        top8 = early_sb("top8", [P, TB, 8])
        idx8 = early_sb("idx8", [P, TB, 8], U32)
        e12 = early_sb("e12", [P, 2, TB])
        l1 = early_sb("l1", [P, NT])
        l2 = early_sb("l2", [P, NT])
        e1 = early_sb("e1", [P, NT])
        e2 = early_sb("e2", [P, NT])
        loc1 = early_sb("loc1", [P, NT])
        rank2 = early_sb("rank2", [P, NT])
        base2 = early_sb("base2", [P, NT])
        loc2 = early_sb("loc2", [P, NT])
        loc4 = early_sb("loc4", [P, 2, TB])
        logit_now = early_sb("logit_now", [P, TB, E])
        mask = early_sb("mask", [P, TB, 2 * E], BF16)
        before = early_sb("before", [P, TB, 2 * E], BF16)
        place = early_sb("place", [P, TB, 2 * CAP], BF16)
        junk = early_sb("junk", [P, 4, P])
        junk_z = early_sb("junk_z", [P, 2, P])
        count1 = early_sb("count1", [P, E])
        ids_hi = early_sb("ids_hi", [P, CAP])
        ids = early_sb("ids", [P, CAP])
        idx_all = early_sb("idx_all", [P, E], I32)
        zsum = early_sb("zsum", [P, NT])
        nmax = early_sb("nmax", [P, NT])
        ga = early_sb("ga", [P, NT])
        gb = early_sb("gb", [P, NT])
        gc = early_sb("gc", [P, NT])
        wexp = early_sb("wexp", [P, EB, KT, D])
        idx_now = early_sb("idx_now", [P, EB], I32)
        rows = early_sb("rows", [P, EB, D])
        rowsT, ysb = xT1, x1
        early.close()

        q_stack = sb("q_stack", [P, 2, H, 2 * P], F32R)
        k_stack = sb("k_stack", [P, 2, H, 2 * P], F32R)
        kq_hi = sb("kq_hi", [P, 2, GRP, 2 * P], F32R)
        kq_lo = sb("kq_lo", [P, 2, GRP, 2 * P], F32R)
        xT_hi = sb("xT_hi", [P, KT, 2 * P], F32R)
        xT_lo = sb("xT_lo", [P, KT, 2 * P], F32R)
        v_sb = sb("v_sb", [P, 4, D])
        xa3 = sb("xa3", [P, 2, 2, D])
        acc = sb("acc", [P, 4, D])
        y1 = sb("y1", [P, 2, D])
        y2 = sb("y2", [P, 2, D])
        probs = sb("probs", [P, 2, 4 * P])
        pT_cur = sb("pT_cur", [P, 2, 4 * P])
        pT_prev = sb("pT_prev", [P, 2, 4 * P])
        o_sb = sb("o_sb", [P, D])
        oT_hi = sb("oT_hi", [P, KT, P], F32R)
        oT_lo = sb("oT_lo", [P, KT, P], F32R)
        mx = sb("mx", [P, 2, 4])
        nmx = sb("nmx", [P, 2, 4])
        psum_row = sb("psum_row", [P, 2, H])
        rsum = sb("rsum", [P, H])
        slot_now = sb("slot_now", [P, 2, 2], I32)

        banks = [ctx.enter_context(nc.psum_tensor(f"bank{k}", [P, 512], F32)) for k in range(8)]
        t_ps, logit_ps, pos_ps, table_ps, y_ps = banks[0:2], banks[2:4], banks[4:6], banks[6], banks[2:4]
        score_ps = [[banks[0], banks[1]], [banks[2], banks[3]]]
        pT_ps, o_ps, unit_ps = banks[4], banks[5], banks[6:8]

        const_made = sem("const_made")
        gvec_in, wgate_in, raw_in = sem("gvec_in"), sem("wgate_in"), sems("raw_in", 2)
        weights_split, raw_scaled, raw_rounded = sem("weights_split"), sem("raw_scaled"), sem("raw_rounded")
        x_in = sems("x_in", TB)
        stat_step, route_step, late_step = sem("stat_step"), sem("route_step"), sem("late_step")
        root_wanted, root_made = sem("root_wanted"), sem("root_made")
        xa_made, xn_scaled, xpx_made = sem("xa_made"), sem("xn_scaled"), sem("xpx_made")
        xa_out, xpx_out = sems("xa_out", TB), sems("xpx_out", TB)
        t_done, xT_made = sem("t_done"), sem("xT_made")
        logits_done, logits_kept, logits_ranked = sem("logits_done"), sem("logits_kept"), sem("logits_ranked")
        mask_made, pos_done, pos_read = sem("mask_made"), sem("pos_done"), sem("pos_read")
        place_made, table_done = sem("place_made"), sem("table_done")
        count_done, place2_made, table2_done = sem("count_done"), sem("place2_made"), sem("table2_done")
        ids_made, idsT_done, idx_made = sem("ids_made"), sem("idsT_done"), sem("idx_made")
        nmax_made, z_made, gate_exp = sem("nmax_made"), sem("z_made"), sem("gate_exp")
        wexp_in, rows_in, ysb_out = sems("wexp_in", EB), sems("rows_in", EB), sems("ysb_out", EB)
        idx_copied, rowsT_done, rowsT_made = sem("idx_copied"), sem("rowsT_done"), sem("rowsT_made")
        y_done, y_copied, routing_made = sem("y_done"), sem("y_copied"), sem("routing_made")
        xa3_in, acc_in, acc_out = sems("xa3_in", 2), sems("acc_in", 4), sems("acc_out", 4)
        y1_in, y2_in, slot_copied = sems("y1_in", 2), sems("y2_in", 2), sem("slot_copied")
        init3 = sem("init3")
        xT_tr, xT_hi_made, xT_split = sem("xT_tr"), sem("xT_hi_made"), sem("xT_split")
        kq_done, kq_hi_made, kq_split = sem("kq_done"), sem("kq_hi_made"), sem("kq_split")
        k_stacked, q_stacked = sem("k_stacked"), sem("q_stacked")
        v_done, v_made = sem("v_done"), sem("v_made")
        score_done, merge_step, nmx_made = sem("score_done"), sem("merge_step"), sem("nmx_made")
        probs_made, pT_done, pT_made = sem("probs_made"), sem("pT_done"), sem("pT_made")
        pv_done, rsum_made, o_made = sem("pv_done"), sem("rsum_made"), sem("o_made")
        oT_tr, oT_hi_made, oT_split = sem("oT_tr"), sem("oT_hi_made"), sem("oT_split")
        h_done, comb_step, fin_done = sem("h_done"), sem("comb_step"), sem("fin_done")

        block = ctx.enter_context(nc.Block())

        def strided(ap, k):
            return ap.rearrange("p (c k) -> p k c", k=KT)[:, k, :]

        CONSTS = 12

        def apart(ins):
            return ins.wait_op(const_made, CONSTS, "sem-ge")

        def experts_done(eng):
            eng.wait_ge(routing_made, 1)
            for b in range(EB):
                eng.wait_ge(ysb_out[b], 16 * NE)

        @block.sync
        def _(sp):
            def load_x(n, j):
                sp.dma_start(x1[:, j, :], x_rows[bass.ds(n * P, P), :]).then_inc(x_in[j], 16)

            for j in range(TB):
                load_x(j, j)
            sp.dma_start(wgate[:, :, :], wg.rearrange("(p k) e -> p k e", k=KT)).then_inc(wgate_in, 16)
            sp.dma_start(gvec[:, :], g.rearrange("(p k) -> p k", k=KT)).then_inc(gvec_in, 16)

            def load_expert(e, b):
                sp.dma_start(wexp[:, b, :, :], we[bass.ds(e, 1), :, :].rearrange("e (p k) f -> p (e k) f", k=KT)).then_inc(wexp_in[b], 16)

            for b in range(EB):
                load_expert(b, b)

            def norm_body(i):
                for j in range(TB):
                    n = i * TB + j
                    wait(sp, xa_made, n + 1)
                    sp.dma_start(xa_rows[bass.ds(n * P, P), :], xa1[:, j, :]).then_inc(xa_out[j], 16)
                    wait(sp, xpx_made, n + 1)
                    sp.dma_start(xpx_rows[bass.ds(n * P, P), :], xp1[:, j, :]).then_inc(xpx_out[j], 16)
                    if not is_last(i, NB):
                        load_x(n + TB, j)

            repeated(sp, NB, norm_body)

            def expert_loads(i):
                for b in range(EB):
                    n = i * EB + b
                    wait(sp, y_done, n + 1)
                    load_expert(n + EB, b)

            with sp.Fori(0, NE - 1) as i:
                expert_loads(i)

            experts_done(sp)

            def load_xa3(pair, h):
                sp.dma_start(xa3[:, h, :, :], xa_rows[bass.ds(pair * 2 * P, 2 * P), :].rearrange("(a p) d -> p a d", p=P)).then_inc(xa3_in[h], 16)

            def load_acc(n, slot):
                sp.dma_start(acc[:, slot, :], xpx_rows[bass.ds(n * P, P), :]).then_inc(acc_in[slot], 16)

            def stack(dst, src, done, h):
                for r in range(4):
                    for q in range(4):
                        sp.dma_start(dst[32 * r:32 * r + 32, h, q::4, :].bitcast(F32),
                                     src[r][32 * q:32 * q + 32, :, :].bitcast(F32)).then_inc(done, 16)

            K_PARTS = [kq_hi[:, 0], kq_lo[:, 0], kq_hi[:, 0], kq_lo[:, 0]]
            Q_PARTS = [kq_hi[:, 1], kq_hi[:, 1], kq_lo[:, 1], kq_lo[:, 1]]

            def stack_pair(pair, h):
                wait(sp, kq_split, pair * 8 + 4)
                wait(sp, score_done, (pair - 1) * 8 + 4)
                stack(k_stack, K_PARTS, k_stacked, h)
                wait(sp, kq_split, pair * 8 + 8)
                stack(q_stack, Q_PARTS, q_stacked, h)

            def store(n, slot):
                wait(sp, fin_done, n * 2 + 2)
                sp.dma_start(out_rows[bass.ds(n * P, P), :], acc[:, slot, :]).then_inc(acc_out[slot], 16)

            load_xa3(0, 0)
            load_xa3(1, 1)
            load_acc(0, 0)
            sp.wait_ge(init3, 2)
            stack_pair(0, 0)

            def pair_body(i, h):
                pair = i * 2 + h
                last = is_last(i, NB)
                if not (last and h == 0 or last and h == 1):
                    wait(sp, xT_tr, pair * 4 + 4)
                    load_xa3(pair + 2, h)
                for n, slot in ((pair * 2 + 1, (2 * h + 1) % 4), (pair * 2 + 2, (2 * h + 2) % 4)):
                    if last and h == 1 and slot == 0:
                        continue
                    k = i if slot > 2 * h else i + 1
                    wait(sp, acc_out[slot], k * 16)
                    load_acc(n, slot)
                if not (last and h == 1):
                    stack_pair(pair + 1, 1 - h)
                if not (is_first(i) and h == 0):
                    store(pair * 2 - 1, (2 * h - 1) % 4)
                store(pair * 2, 2 * h)

            def body(i):
                for h in range(2):
                    pair_body(i, h)

            repeated(sp, NB, body)
            store(NT - 1, 3)
            for k in range(4):
                sp.wait_ge(acc_out[k], 16 * NB)

        @block.gpsimd
        def _(pool):
            gp = nc.gpsimd
            gp.memset(ident[:, :], 0.0).then_inc(const_made, 1)
            gp.memset(tri[:, :], 1.0).then_inc(const_made, 1)
            gp.memset(ones[:, :], 1.0).then_inc(const_made, 1)
            gp.memset(zeros[:, :], 0.0).then_inc(const_made, 1)
            gp.memset(keep_cur[:, :], 1.0).then_inc(const_made, 1)
            gp.memset(keep_prev[:, :], 1.0).then_inc(const_made, 1)
            gp.iota(iota_row[:, :], [[1, P]], base=0, channel_multiplier=0, allow_small_or_imprecise_dtypes=True).then_inc(const_made, 1)
            gp.iota(tile_no[:, :], [[1, NT]], base=0, channel_multiplier=0, allow_small_or_imprecise_dtypes=True).then_inc(const_made, 1)
            gp.iota(lane[:, :], [[1, 1]], base=0, channel_multiplier=1, allow_small_or_imprecise_dtypes=True).then_inc(const_made, 1)
            gp.memset(prev_cap[:, :], -MASKED).then_inc(const_made, 1)
            gp.memset(above[:, :, :], 1).then_inc(const_made, 1)
            gp.memset(before[:, 0, :], 0.0).then_inc(const_made, 1)
            pool.wait_ge(const_made, CONSTS)
            gp.affine_select(out=ident[:, :], in_=ident[:, :], compare_op=ALU.not_equal, fill=1.0, base=0,
                             pattern=[[-1, P]], channel_multiplier=1).then_inc(const_made, 1)
            gp.affine_select(out=tri[:, :], in_=tri[:, :], compare_op=ALU.is_gt, fill=0.0, base=0,
                             pattern=[[1, P]], channel_multiplier=-1).then_inc(const_made, 1)
            gp.affine_select(out=keep_cur[:, :], in_=keep_cur[:, :], compare_op=ALU.is_ge, fill=0.0, base=0,
                             pattern=[[0, 4], [1, P]], channel_multiplier=-1).then_inc(const_made, 1)
            gp.affine_select(out=keep_prev[:, :], in_=keep_prev[:, :], compare_op=ALU.is_gt, fill=0.0, base=0,
                             pattern=[[0, 4], [-1, P]], channel_multiplier=1).then_inc(const_made, 1)
            gp.affine_select(out=above[:, :, :], in_=above[:, :, :], compare_op=ALU.is_gt, fill=0.0, base=0,
                             pattern=[[0, 4], [1, P]], channel_multiplier=-1).then_inc(const_made, 1)
            for b in range(B):
                gp.memset(prev_cap[:, b * PER_SEQ:b * PER_SEQ + 1], MASKED).then_inc(const_made, 1)

            def load_raw(c):
                if c < KT:
                    pool.dma_start(raw[:, c % 2, 0:3 * D], wqkv.rearrange("(p k) n -> p k n", k=KT)[:, c, :]).then_inc(raw_in[c % 2], 16)
                else:
                    pool.dma_start(raw[:, c % 2, :], wo.rearrange("(p k) n -> p (k n)", k=KT)).then_inc(raw_in[c % 2], 16)

            def split_raw(c):
                pool.wait_ge(raw_in[c % 2], 16 * (c // 2 + 1))
                if c < KT:
                    part, hi, lo = raw[:, c % 2, 0:3 * D], wqkv_hi[:, c, :], wqkv_lo[:, c, :]
                    gp.tensor_scalar(part, part, gvec[:, c:c + 1], None, ALU.mult).then_inc(raw_scaled, 1)
                    pool.wait_ge(raw_scaled, c + 1)
                else:
                    part, hi, lo = raw[:, c % 2, :], wo_hi[:, :, :].rearrange("p k n -> p (k n)"), wo_lo[:, :, :].rearrange("p k n -> p (k n)")
                gp.tensor_copy(hi, part).then_inc(raw_rounded, 1)
                pool.wait_ge(raw_rounded, c + 1)
                gp.tensor_tensor(lo, part, hi.bitcast(F32), ALU.subtract).then_inc(weights_split, 1)
                pool.wait_ge(weights_split, c + 1)

            pool.wait_ge(gvec_in, 16)
            load_raw(0)
            load_raw(1)

            def norm_body(i):
                for j in range(TB):
                    n = i * TB + j
                    wait(pool, xa_made, n + 1)
                    wait(pool, xpx_out[j], i * 16)
                    gp.tensor_tensor(xp1[:, j, :], xa1[:, j, :], ir2[:, bass.ds(n, 1)].to_broadcast([P, D]), ALU.mult).then_inc(xn_scaled, 1)
                    wait(pool, xn_scaled, n + 1)
                    gp.tensor_tensor(xp1[:, j, :], xp1[:, j, :], x1[:, j, :], ALU.add).then_inc(xpx_made, 1)

            repeated(pool, NB, norm_body)
            for c in range(KT + 1):
                split_raw(c)
                if c + 2 <= KT:
                    load_raw(c + 2)

            for j in range(TB):
                pool.wait_ge(xa_out[j], 16 * NB)
            pool.wait_ge(idx_made, 1)

            def expert_body(i):
                for b in range(EB):
                    n = i * EB + b
                    wait(pool, rows_in[b], i * 16)
                    wait(pool, rowsT_done, n + 1 - EB)
                    gp.tensor_copy(idx_now[:, b:b + 1], idx_all[:, bass.ds(n, 1)]).then_inc(idx_copied, 1)
                    wait(pool, idx_copied, n + 1)
                    apart(gp.indirect_dma_start(rows[:, b, :], None, xa_rows[:, :],
                                          bass.IndirectOffsetOnAxis(ap=idx_now[:, b:b + 1], axis=0))).then_inc(rows_in[b], 16)

            repeated(pool, NE, expert_body)

            experts_done(pool)
            gp.memset(v_sb[:, 3, :], 0.0).then_inc(init3, 1)
            gp.memset(k_stack[:, 1, :, :].bitcast(F32), 0.0).then_inc(init3, 1)

            def gather_body(i):
                for j in range(TB):
                    n, a = i * TB + j, j % 2
                    wait(pool, comb_step, (n - 1) * 2)
                    gp.tensor_copy(slot_now[:, a, 0:1], slot1[:, bass.ds(n, 1)]).then_inc(slot_copied, 1)
                    gp.tensor_copy(slot_now[:, a, 1:2], slot2[:, bass.ds(n, 1)]).then_inc(slot_copied, 1)
                    wait(pool, slot_copied, n * 2 + 2)
                    apart(gp.indirect_dma_start(y1[:, a, :], None, yb_rows[:, :],
                                          bass.IndirectOffsetOnAxis(ap=slot_now[:, a, 0:1], axis=0))).then_inc(y1_in[a], 16)
                    apart(gp.indirect_dma_start(y2[:, a, :], None, yb_rows[:, :],
                                          bass.IndirectOffsetOnAxis(ap=slot_now[:, a, 1:2], axis=0))).then_inc(y2_in[a], 16)

            repeated(pool, NB, gather_body)

        SCHEDULE = [
            [("xT", 0, 0), ("xT", 0, 1), ("xT", 1, 0), ("xT", 1, 1)],
            [("kq", 0, 0), ("kq", 0, 1), ("kq", 0, 2)],
            [("kq", 0, 3), ("kq", 1, 0), ("kq", 1, 1)],
            [("kq", 1, 2), ("kq", 1, 3), ("oT", 1, 0), ("oT", 1, 1)],
            [("wo", 1, 0), ("wo", 1, 1), ("v", 0, 0)],
            [("v", 0, 1), ("v", 1, 0)],
            [("oT", 0, 0), ("oT", 0, 1), ("v", 1, 1)],
            [("wo", 0, 0), ("wo", 0, 1)],
        ]
        UNITS = [u for step in SCHEDULE for u in step]
        PROJECTION = [u for u in UNITS if u[0] in ("xT", "kq", "v")]
        assert len(UNITS) == 24

        def unit_exists(unit, i, h):
            kind, a, _ = unit
            if kind in ("xT", "kq", "v"):
                return not (is_last(i, NB) and h == 1)
            return not (a == 1 and is_first(i) and h == 0)

        def unit_index(unit, pair):
            kind, a, c = unit
            if kind == "xT" or kind == "v":
                return pair * 4 + 4 + 2 * a + c
            if kind == "kq":
                return pair * 8 + 8 + 4 * a + c
            n = pair * 2 - 1 if a == 1 else pair * 2
            return n * 2 + c

        CONSUMED = {"xT": xT_split, "kq": kq_split, "v": v_made, "oT": oT_split, "wo": fin_done}

        @block.tensor
        def _(pe):
            mm = nc.tensor.matmul

            pe.wait_ge(const_made, CONSTS + 5)
            pe.wait_ge(wgate_in, 16)
            mm(table_ps[:, 0:2 * CAP], zeros[:, 0:P], zeros[:, :], start=True, stop=True)

            def transposes(i, j):
                n = i * TB + j
                wait(pe, xa_made, n + 1)
                wait(pe, xT_made, n - 1)
                for k in range(KT):
                    ins = nc.tensor.transpose(t_ps[j % 2][:, k * P:(k + 1) * P], strided(xa1[:, j, :], k), ident[:, :])
                ins.then_inc(t_done, 1)

            def logits(i, j):
                n = i * TB + j
                wait(pe, xT_made, n + 1)
                wait(pe, logits_kept, n - 1)
                for k in range(KT):
                    ins = mm(logit_ps[j % 2][:, 0:E], xT1[:, j % 2, k, :], wgate[:, k, :], start=(k == 0), stop=(k == KT - 1))
                ins.then_inc(logits_done, 1)

            def positions(i, j):
                n = i * TB + j
                wait(pe, mask_made, n + 1)
                wait(pe, pos_read, n - 1)
                mm(pos_ps[j % 2][:, 0:2 * E], tri[:, :], mask[:, j, :], start=True, stop=False)
                mm(pos_ps[j % 2][:, 0:2 * E], ones[:, :], before[:, j, :], start=False, stop=True).then_inc(pos_done, 1)

            def table(sem_ready, sem_done, first_col, i, j):
                wait(pe, sem_ready, i * TB + j + 1)
                mm(table_ps[:, 0:2 * CAP], mask[:, j, first_col:first_col + E], place[:, j, :], start=False, stop=True,
                   skip_group_check=True).then_inc(sem_done, 1)

            def front(i):
                for j in range(TB):
                    transposes(i, j)
                    if j:
                        logits(i, j - 1)
                logits(i, TB - 1)

            front(0)

            def norm_body(i):
                if not is_last(i, NB):
                    front(i + 1)
                for j in range(TB):
                    positions(i, j)
                for j in range(TB):
                    table(place_made, table_done, 0, i, j)

            repeated(pe, NB, norm_body)
            mm(pos_ps[0][:, 0:2 * E], ones[:, :], before[:, 0, :], start=True, stop=True).then_inc(count_done, 1)

            def second_body(i):
                for j in range(TB):
                    table(place2_made, table2_done, E, i, j)

            repeated(pe, NB, second_body)
            pe.wait_ge(ids_made, 1)
            nc.tensor.transpose(pos_ps[1][:, 0:P], ids[:, :], ident[:, :]).then_inc(idsT_done, 1)

            def rows_transposed(n, b, i):
                wait(pe, rows_in[b], i * 16 + 16)
                wait(pe, rowsT_made, n - 1)
                for k in range(KT):
                    ins = nc.tensor.transpose(t_ps[b % 2][:, k * P:(k + 1) * P], strided(rows[:, b, :], k), ident[:, :])
                ins.then_inc(rowsT_done, 1)

            def expert_product(n, b, i):
                wait(pe, rowsT_made, n + 1)
                wait(pe, wexp_in[b], i * 16 + 16)
                wait(pe, y_copied, n - 1)
                for k in range(KT):
                    ins = mm(y_ps[b % 2][:, :], rowsT[:, b % 2, k, :], wexp[:, b, k, :], start=(k == 0), stop=(k == KT - 1))
                ins.then_inc(y_done, 1)

            rows_transposed(0, 0, 0)

            def expert_body(i):
                for b in range(EB):
                    n = i * EB + b
                    if not (is_last(i, NE) and b == EB - 1):
                        rows_transposed(n + 1, (b + 1) % EB, i + (b + 1) // EB)
                    expert_product(n, b, i)

            repeated(pe, NE, expert_body)

            experts_done(pe)
            pe.wait_ge(weights_split, KT + 1)

            def half(u):
                return unit_ps[u % 2][:, 0:256]

            def split_product(dst, left_hi, left_lo, right_hi, right_lo, done):
                for k in range(KT):
                    for p, (a, b) in enumerate(((left_hi, right_hi), (left_hi, right_lo), (left_lo, right_hi))):
                        ins = mm(dst, a(k), b(k), start=(k == 0 and p == 0), stop=(k == KT - 1 and p == 2))
                ins.then_inc(done, 1)

            def run_unit(unit, u, pair, h):
                kind, a, c = unit
                n = pair * 2 - 1 if a == 1 else pair * 2
                dst = half(u)
                if kind == "xT":
                    if (a, c) == (0, 0):
                        wait(pe, xa3_in[1 - h], unit_rounds(pair, h))
                    for k in range(2):
                        ins = nc.tensor.transpose(dst[:, k * P:(k + 1) * P], strided(xa3[:, 1 - h, a, :], 2 * c + k), ident[:, :])
                    ins.then_inc(xT_tr, 1)
                elif kind == "kq":
                    if (a, c) == (0, 0):
                        wait(pe, xT_split, pair * 4 + 8)
                    col = (D if a == 0 else 0) + c * P
                    split_product(dst, lambda k: wqkv_hi[:, k, col:col + P], lambda k: wqkv_lo[:, k, col:col + P],
                                  lambda k: xT_hi[:, k, :], lambda k: xT_lo[:, k, :], kq_done)
                elif kind == "v":
                    col = 2 * D + c * 256
                    split_product(dst, lambda k: xT_hi[:, k, a * P:(a + 1) * P], lambda k: xT_lo[:, k, a * P:(a + 1) * P],
                                  lambda k: wqkv_hi[:, k, col:col + 256], lambda k: wqkv_lo[:, k, col:col + 256], v_done)
                elif kind == "oT":
                    wait(pe, o_made, n + 1)
                    for k in range(2):
                        ins = nc.tensor.transpose(dst[:, k * P:(k + 1) * P], strided(o_sb[:, :], 2 * c + k), ident[:, :])
                    ins.then_inc(oT_tr, 1)
                else:
                    wait(pe, oT_split, n * 2 + 2)
                    col = c * 256
                    split_product(dst, lambda k: oT_hi[:, k, :], lambda k: oT_lo[:, k, :],
                                  lambda k: wo_hi[:, k, col:col + 256], lambda k: wo_lo[:, k, col:col + 256], h_done)

            def unit_rounds(pair, h):
                return ((pair - h) // 2 if isinstance(pair, int) else body_of[0]) * 16 + (16 if h == 0 else 32)

            body_of = [0]

            def scores(i, h, s):
                if s == 8:
                    i, h, s = (i, 1, 0) if h == 0 else (i + 1, 0, 0)
                pair = i * 2 + h
                step, a, grp = pair * 8 + s, s // 4, s % 4
                if s == 0:
                    wait(pe, k_stacked, (pair + 1) * 256)
                    wait(pe, q_stacked, (pair + 1) * 256)
                wait(pe, probs_made, step - 1)
                dst_prev, dst_cur = score_ps[s % 2]
                for hh in range(4):
                    head = grp * 4 + hh
                    q_part = q_stack[:, h, head, a * P:(a + 1) * P]
                    k_prev = k_stack[:, h, head, 0:P] if a == 1 else k_stack[:, 1 - h, head, P:2 * P]
                    mm(dst_cur[:, hh * P:(hh + 1) * P], q_part, k_stack[:, h, head, a * P:(a + 1) * P], start=True, stop=True)
                    ins = mm(dst_prev[:, hh * P:(hh + 1) * P], q_part, k_prev, start=True, stop=True)
                ins.then_inc(score_done, 1)

            def values(i, h, s):
                if s == -1:
                    if is_first(i) and h == 0:
                        return
                    i, h, s = (i, 0, 7) if h == 1 else (i - 1, 1, 7)
                step, a, grp = (i * 2 + h) * 8 + s, s // 4, s % 4
                n = (i * 2 + h) * 2 + a
                slot = 2 * h + a
                wait(pe, pT_made, step + 1)
                if grp == 0:
                    wait(pe, v_made, n * 2 + 2)
                    wait(pe, o_made, n)
                for hh in range(4):
                    head = grp * 4 + hh
                    cols = slice(head * DH, (head + 1) * DH)
                    mm(o_ps[:, cols], pT_cur[:, s % 2, hh * P:(hh + 1) * P], v_sb[:, slot, cols], start=True, stop=False)
                    ins = mm(o_ps[:, cols], pT_prev[:, s % 2, hh * P:(hh + 1) * P], v_sb[:, (slot - 1) % 4, cols], start=False, stop=True)
                ins.then_inc(pv_done, 1)

            def probs_transposed(i, h, s):
                step = (i * 2 + h) * 8 + s
                wait(pe, probs_made, step + 1)
                wait(pe, pT_made, step)
                for hh in range(4):
                    ins = nc.tensor.transpose(pT_ps[:, hh * P:(hh + 1) * P], probs[:, s % 2, hh * P:(hh + 1) * P], ident[:, :])
                ins.then_inc(pT_done, 1)

            held = [None, None]

            def run_units(units, pair, h, i):
                for u, unit in units:
                    if not unit_exists(unit, i, h):
                        continue
                    if held[u % 2] is not None:
                        wait(pe, *held[u % 2])
                    run_unit(unit, u, pair, h)
                    held[u % 2] = (CONSUMED[unit[0]], unit_index(unit, pair) + 1)

            body_of[0] = -1
            run_units(list(enumerate(PROJECTION)), -1, 1, -1)
            pe.wait_ge(init3, 2)
            scores(0, 0, 0)

            def body(i):
                body_of[0] = i
                if not is_first(i):
                    for u in (22, 23):
                        held[u % 2] = (CONSUMED[UNITS[u][0]], unit_index(UNITS[u], i * 2 - 1) + 1)
                for h in range(2):
                    pair, u = i * 2 + h, 0
                    for s in range(8):
                        if not (is_last(i, NB) and h == 1 and s == 7):
                            scores(i, h, s + 1)
                        values(i, h, s - 1)
                        probs_transposed(i, h, s)
                        run_units(list(enumerate(SCHEDULE[s], u)), pair, h, i)
                        u += len(SCHEDULE[s])

            repeated(pe, NB, body)
            values(NB - 1, 1, 7)
            for unit in (("oT", 1, 0), ("oT", 1, 1), ("wo", 1, 0), ("wo", 1, 1)):
                u = unit[2]
                wait(pe, *held[u % 2])
                run_unit(unit, u, NP, 0)
                held[u % 2] = (CONSUMED[unit[0]], unit_index(unit, NP) + 1)

        @block.scalar
        def _(act):
            sc = nc.scalar

            def roots(i):
                for r in range(2):
                    wait(act, root_wanted, i * 2 + r + 1)
                    sc.activation(root[:, :], ve[:, :], ACT.Sqrt).then_inc(root_made, 1)

            def front(i):
                for j in range(TB):
                    n = i * TB + j
                    wait(act, t_done, n + 1)
                    wait(act, logits_done, n - 1)
                    sc.activation(xT1[:, j % 2, :, :], t_ps[j % 2][:, :], ACT.Copy).then_inc(xT_made, 1)
                    if j:
                        keep(i, j - 1)
                keep(i, TB - 1)

            def keep(i, j):
                n = i * TB + j
                wait(act, logits_done, n + 1)
                sc.activation(logit_all[:, bass.ds(n, 1), :], logit_ps[j % 2][:, 0:E], ACT.Copy)
                wait(act, logits_ranked, n + 1 - TB)
                sc.activation(logit_now[:, j, :], logit_ps[j % 2][:, 0:E], ACT.Copy).then_inc(logits_kept, 1)

            roots(0)
            front(0)

            def norm_body(i):
                if not is_last(i, NB):
                    roots(i + 1)
                    front(i + 1)

            repeated(act, NB, norm_body)

            act.wait_ge(nmax_made, 2)
            act.wait_ge(logits_kept, NT)

            def sums(i):
                for j in range(TB):
                    n = i * TB + j
                    if j >= 2:
                        wait(act, z_made, n - 1)
                    elif not is_first(i):
                        wait(act, z_made, n - 1)
                    sc.activation(junk_z[:, j % 2, :], logit_all[:, bass.ds(n, 1), :], ACT.Exp, bias=nmax[:, bass.ds(n, 1)],
                                  scale=ir2[:, bass.ds(n, 1)], accum_out=zsum[:, bass.ds(n, 1)]).then_inc(z_made, 1)

            repeated(act, NB, sums)
            sc.activation(gb[:, :], ga[:, :], ACT.Exp).then_inc(gate_exp, 1)

            def expert_body(i):
                for b in range(EB):
                    n = i * EB + b
                    wait(act, y_done, n + 1)
                    wait(act, ysb_out[b], i * 16)
                    sc.activation(ysb[:, b, :], y_ps[b % 2][:, :], ACT.Copy).then_inc(y_copied, 1)
                    wait(act, y_copied, n + 1)
                    act.dma_start(yb_rows[bass.ds(n * P, P), :], ysb[:, b, :]).then_inc(ysb_out[b], 16)

            repeated(act, NE, expert_body)

            experts_done(act)

            def half(u):
                return unit_ps[u % 2][:, 0:256]

            def read_unit(unit, u, pair):
                kind, a, c = unit
                idx = unit_index(unit, pair)
                if kind == "xT":
                    wait(act, xT_tr, idx + 1)
                    sc.activation(xT_hi[:, 2 * c:2 * c + 2, a * P:(a + 1) * P], half(u), ACT.Copy).then_inc(xT_hi_made, 1)
                elif kind == "kq":
                    wait(act, kq_done, idx + 1)
                    if c == 0:
                        wait(act, (k_stacked, q_stacked)[a], (pair + 1) * 256)
                    sc.activation(kq_hi[:, a, c, :], half(u), ACT.Copy).then_inc(kq_hi_made, 1)
                elif kind == "v":
                    wait(act, v_done, idx + 1)
                    slot = v_slot(pair, a)
                    sc.activation(v_sb[:, slot, c * 256:(c + 1) * 256], half(u), ACT.Copy).then_inc(v_made, 1)
                elif kind == "oT":
                    wait(act, oT_tr, idx + 1)
                    wait(act, h_done, idx - c)
                    sc.activation(oT_hi[:, 2 * c:2 * c + 2, :], half(u), ACT.Copy).then_inc(oT_hi_made, 1)

            h_now = [0]

            def v_slot(pair, a):
                return 2 * (1 - h_now[0]) + a

            def exps(i, h, s):
                if s == 8:
                    i, h, s = (i, 1, 0) if h == 0 else (i + 1, 0, 0)
                step, a, grp = (i * 2 + h) * 8 + s, s // 4, s % 4
                n = (i * 2 + h) * 2 + a
                wait(act, nmx_made, step + 1)
                wait(act, pT_done, step - 1)
                if grp == 0:
                    wait(act, rsum_made, n - 1)
                for hh in range(4):
                    ins = sc.activation(probs[:, s % 2, hh * P:(hh + 1) * P], score_ps[s % 2][1][:, hh * P:(hh + 1) * P], ACT.Exp,
                                        bias=nmx[:, s % 2, hh:hh + 1], scale=SCALE,
                                        accum_out=psum_row[:, a, grp * 4 + hh:grp * 4 + hh + 1])
                ins.then_inc(probs_made, 1)

            h_now[0] = 1
            for u, unit in enumerate(PROJECTION):
                read_unit(unit, u, -1)
            exps(0, 0, 0)

            def body(i):
                for h in range(2):
                    h_now[0] = h
                    pair, u = i * 2 + h, 0
                    for s in range(8):
                        if not (is_last(i, NB) and h == 1 and s == 7):
                            exps(i, h, s + 1)
                        for unit in SCHEDULE[s]:
                            if unit_exists(unit, i, h):
                                read_unit(unit, u, pair)
                            u += 1

            repeated(act, NB, body)
            for c in range(2):
                read_unit(("oT", 1, c), c, NP)

        @block.vector
        def _(dve):
            ve_ = nc.vector
            STATS, ROUTE = 20, 24

            def newton(chain, y, v):
                chain.settle()
                chain.did(ve_.scalar_tensor_tensor(tmp4[:, :], y[:, :], -0.5, y[:, :], ALU.mult, ALU.mult))
                chain.settle()
                chain.did(ve_.tensor_tensor(tmp4[:, :], tmp4[:, :], v[:, :], ALU.mult))
                chain.settle()
                chain.did(ve_.scalar_tensor_tensor(y[:, :], tmp4[:, :], 1.5, y[:, :], ALU.add, ALU.mult))

            def stats(i):
                chain = Chain(dve, stat_step, i * STATS)
                for j in range(TB):
                    wait(dve, x_in[j], i * 16 + 16)
                    chain.did(ve_.bn_stats(bn6[:, j, :], x1[:, j, :]))
                chain.settle()
                for j in range(TB):
                    chain.did(apart(ve_.bn_aggr(mv[:, j, :], bn6[:, j, :])))
                chain.settle()
                ve_.tensor_scalar(ve[:, :], mv[:, :, 1], LN_EPS, None, ALU.add).then_inc(root_wanted, 1)
                wait(dve, root_made, i * 2 + 1)
                chain.did(ve_.reciprocal(rstd[:, :], root[:, :]))
                newton(chain, rstd, ve)
                chain.settle()
                chain.did(ve_.tensor_tensor(ms[:, :], rstd[:, :], rstd[:, :], ALU.mult))
                chain.settle()
                chain.did(ve_.tensor_tensor(ms[:, :], ms[:, :], mv[:, :, 1], ALU.mult))
                chain.settle()
                ve_.tensor_scalar(ve[:, :], ms[:, :], RMS_EPS, None, ALU.add).then_inc(root_wanted, 1)
                wait(dve, root_made, i * 2 + 2)
                chain.did(ve_.reciprocal(r2[:, :], root[:, :]))
                newton(chain, r2, ve)
                chain.settle()
                chain.did(ve_.tensor_tensor(comb[:, :], rstd[:, :], r2[:, :], ALU.mult))
                chain.did(ve_.tensor_tensor(ir2[:, bass.ds(i * TB, TB)], ve[:, :], r2[:, :], ALU.mult))
                chain.settle()
                for j in range(TB):
                    n = i * TB + j
                    wait(dve, xa_out[j], i * 16)
                    wait(dve, xpx_made, n + 1 - TB)
                    wait(dve, t_done, n + 1 - TB)
                    ve_.tensor_scalar(xa1[:, j, :], x1[:, j, :], mv[:, j, 0:1], comb[:, j:j + 1], ALU.subtract, ALU.mult).then_inc(xa_made, 1)
                wait(dve, xa_made, (i + 1) * TB)
                assert chain.n == STATS, chain.n

            def onehots(chain, i, j, col, value, dst):
                return ve_.tensor_scalar(dst, iota_row[:, :], value, None, ALU.is_equal)

            def route(i):
                chain = Chain(dve, route_step, i * ROUTE)
                now = bass.ds(i * TB, TB)
                for j in range(TB):
                    wait(dve, logits_kept, i * TB + j + 1)
                    chain.did(apart(ve_.max(top8[:, j, :], logit_now[:, j, :])))
                chain.settle()
                for j in range(TB):
                    apart(ve_.max_index(idx8[:, j, :], top8[:, j, :], logit_now[:, j, :])).then_inc(logits_ranked, 1)
                wait(dve, logits_ranked, (i + 1) * TB)
                for c, (keep_e, keep_l) in enumerate(((e1, l1), (e2, l2))):
                    chain.did(ve_.tensor_copy(e12[:, c, :], idx8[:, :, c]))
                    chain.did(ve_.tensor_copy(keep_e[:, now], idx8[:, :, c]))
                    chain.did(ve_.tensor_copy(keep_l[:, now], top8[:, :, c]))
                chain.settle()
                for j in range(TB):
                    n = i * TB + j
                    wait(dve, table_done, n + 1 - TB)
                    for c in range(2):
                        chain.did(ve_.tensor_scalar(mask[:, j, c * E:(c + 1) * E], iota_row[:, :], e12[:, c, j:j + 1], None, ALU.is_equal))
                    if j == TB - 1:
                        wait(dve, mask_made, i * TB + j)
                        wait(dve, pos_done, i * TB + 1)
                    chain.settle()
                    if j:
                        wait(dve, mask_made, n)
                    elif not is_first(i):
                        wait(dve, mask_made, i * TB)
                    ve_.tensor_tensor(before[:, (j + 1) % TB, :], before[:, j, :], mask[:, j, :], ALU.add).then_inc(mask_made, 1)
                for j in range(TB):
                    n = i * TB + j
                    wait(dve, pos_done, n + 1)
                    chain.did(ve_.scalar_tensor_tensor(junk[:, j, :], pos_ps[j % 2][:, 0:E], 1.0, mask[:, j, 0:E], ALU.mult, ALU.mult,
                                                       accum_out=loc4[:, 0, j:j + 1]))
                    chain.settle()
                    ve_.scalar_tensor_tensor(junk[:, j, :], pos_ps[j % 2][:, E:2 * E], 1.0, mask[:, j, E:2 * E], ALU.mult, ALU.mult,
                                             accum_out=loc4[:, 1, j:j + 1]).then_inc(pos_read, 1)
                wait(dve, pos_read, (i + 1) * TB)
                for j in range(TB):
                    n = i * TB + j
                    ve_.tensor_scalar(place[:, j, 0:CAP], iota_row[:, :], loc4[:, 0, j:j + 1], lane[:, :], ALU.is_equal, ALU.mult)
                    ve_.tensor_scalar(place[:, j, CAP:2 * CAP], iota_row[:, :], loc4[:, 0, j:j + 1], tile_no[:, bass.ds(n, 1)],
                                      ALU.is_equal, ALU.mult).then_inc(place_made, 1)
                chain.did(ve_.tensor_copy(loc1[:, now], loc4[:, 0, :]))
                chain.did(ve_.tensor_copy(rank2[:, now], loc4[:, 1, :]))
                wait(dve, place_made, (i + 1) * TB)
                chain.settle()
                assert chain.n == ROUTE, chain.n

            dve.wait_ge(const_made, CONSTS + 5 + B)
            stats(0)

            def norm_body(i):
                if not is_last(i, NB):
                    stats(i + 1)
                route(i)

            repeated(dve, NB, norm_body)

            dve.wait_ge(count_done, 1)
            late = Chain(dve, late_step, 0)
            late.did(ve_.tensor_copy(count1[:, :], pos_ps[0][:, 0:E]))
            late.did(ve_.tensor_tensor(gc[:, :], l2[:, :], l1[:, :], ALU.subtract))
            ve_.scalar_tensor_tensor(nmax[:, :], l1[:, :], -1.0, ir2[:, :], ALU.mult, ALU.mult).then_inc(nmax_made, 1)
            late.settle()
            ve_.tensor_tensor(ga[:, :], gc[:, :], ir2[:, :], ALU.mult).then_inc(nmax_made, 1)
            BASE = late.n

            def second_places(i):
                chain = Chain(dve, late_step, i * 3 * TB + BASE)
                for j in range(TB):
                    n = i * TB + j
                    chain.did(ve_.scalar_tensor_tensor(junk[:, j, :], iota_row[:, :], e2[:, bass.ds(n, 1)], count1[:, :],
                                                       ALU.is_equal, ALU.mult, accum_out=base2[:, bass.ds(n, 1)]))
                chain.settle()
                for j in range(TB):
                    n = i * TB + j
                    chain.did(ve_.tensor_tensor(loc2[:, bass.ds(n, 1)], base2[:, bass.ds(n, 1)], rank2[:, bass.ds(n, 1)], ALU.add))
                chain.settle()
                for j in range(TB):
                    n = i * TB + j
                    if is_first(i):
                        wait(dve, table_done, NT)
                    wait(dve, table2_done, n + 1 - TB)
                    chain.did(ve_.tensor_scalar(mask[:, j, E:2 * E], iota_row[:, :], e2[:, bass.ds(n, 1)], None, ALU.is_equal))
                    ve_.tensor_scalar(place[:, j, 0:CAP], iota_row[:, :], loc2[:, bass.ds(n, 1)], lane[:, :], ALU.is_equal, ALU.mult)
                    ve_.tensor_scalar(place[:, j, CAP:2 * CAP], iota_row[:, :], loc2[:, bass.ds(n, 1)], tile_no[:, bass.ds(n, 1)],
                                      ALU.is_equal, ALU.mult).then_inc(place2_made, 1)
                chain.settle()

            repeated(dve, NB, second_places)
            dve.wait_ge(table2_done, NT)
            late = Chain(dve, late_step, BASE + 3 * TB * NB)
            late.did(ve_.tensor_scalar(ids_hi[:, :], table_ps[:, CAP:2 * CAP], float(P), None, ALU.mult))
            late.settle()
            ve_.tensor_tensor(ids[:, :], table_ps[:, 0:CAP], ids_hi[:, :], ALU.add).then_inc(ids_made, 1)
            dve.wait_ge(idsT_done, 1)
            ve_.tensor_copy(idx_all[:, :], pos_ps[1][:, 0:P]).then_inc(idx_made, 1)

            def expert_body(i):
                for b in range(EB):
                    n = i * EB + b
                    wait(dve, rowsT_done, n + 1)
                    wait(dve, y_done, n - 1)
                    ve_.tensor_copy(rowsT[:, b % 2, :, :], t_ps[b % 2][:, :].rearrange("p (k c) -> p k c", k=KT)).then_inc(rowsT_made, 1)

            repeated(dve, NE, expert_body)

            dve.wait_ge(z_made, NT)
            dve.wait_ge(gate_exp, 1)

            def step(ins):
                late.did(ins)
                late.settle()

            step(ve_.reciprocal(ga[:, :], zsum[:, :]))
            step(ve_.tensor_tensor(gb[:, :], gb[:, :], ga[:, :], ALU.mult))
            step(ve_.tensor_tensor(gc[:, :], ga[:, :], gb[:, :], ALU.add))
            step(ve_.tensor_scalar(gc[:, :], gc[:, :], GATE_EPS, None, ALU.max))
            step(ve_.reciprocal(zsum[:, :], gc[:, :]))
            step(ve_.tensor_tensor(zsum[:, :], zsum[:, :], ir2[:, :], ALU.mult))
            for gate, e, loc, weight, slot in ((ga, e1, loc1, w1, slot1), (gb, e2, loc2, w2, slot2)):
                step(ve_.tensor_tensor(gate[:, :], gate[:, :], zsum[:, :], ALU.mult))
                step(ve_.tensor_scalar(gc[:, :], loc[:, :], float(CAP), None, ALU.is_lt))
                step(ve_.tensor_tensor(weight[:, :], gate[:, :], gc[:, :], ALU.mult))
                step(ve_.tensor_scalar(gc[:, :], loc[:, :], float(CAP - 1), None, ALU.min))
                step(ve_.scalar_tensor_tensor(gate[:, :], e[:, :], float(CAP), gc[:, :], ALU.mult, ALU.add))
                step(ve_.tensor_copy(slot[:, :], gate[:, :]))
            ve_.memset(tmp4[:, :], 0.0).then_inc(routing_made, 1)

            experts_done(dve)

            def half(u):
                return unit_ps[u % 2][:, 0:256]

            def read_unit(unit, u, pair):
                kind, a, c = unit
                idx = unit_index(unit, pair)
                if kind == "xT":
                    wait(dve, xT_hi_made, idx + 1)
                    part = slice(2 * c, 2 * c + 2), slice(a * P, (a + 1) * P)
                    ve_.tensor_tensor(xT_lo[:, part[0], part[1]], half(u).rearrange("p (k c) -> p k c", k=2),
                                      xT_hi[:, part[0], part[1]].bitcast(F32), ALU.subtract).then_inc(xT_split, 1)
                elif kind == "kq":
                    wait(dve, kq_hi_made, idx + 1)
                    ve_.tensor_tensor(kq_lo[:, a, c, :], half(u), kq_hi[:, a, c, :].bitcast(F32), ALU.subtract).then_inc(kq_split, 1)
                elif kind == "oT":
                    wait(dve, oT_hi_made, idx + 1)
                    ve_.tensor_tensor(oT_lo[:, 2 * c:2 * c + 2, :], half(u).rearrange("p (k c) -> p k c", k=2),
                                      oT_hi[:, 2 * c:2 * c + 2, :].bitcast(F32), ALU.subtract).then_inc(oT_split, 1)
                elif kind == "wo":
                    wait(dve, h_done, idx + 1)
                    slot = (2 * h_now[0] + (0 if a == 0 else -1)) % 4
                    cols = slice(c * 256, (c + 1) * 256)
                    ve_.tensor_tensor(acc[:, slot, cols], half(u), acc[:, slot, cols], ALU.add).then_inc(fin_done, 1)

            h_now = [0]
            MERGE = 2 * 16 + 4

            def merge(i, h, s, chain):
                if s == 8:
                    if h == 0:
                        h, s = 1, 0
                    else:
                        i, h, s = i + 1, 0, 0
                step, a = (i * 2 + h) * 8 + s, s // 4
                prev, cur = score_ps[s % 2]
                wait(dve, score_done, step + 1)
                if h == 0 and a == 0:
                    chain.did(ve_.tensor_scalar(prev[:, :], prev[:, :], prev_cap[:, bass.ds(i, 1)], None, ALU.min))
                    chain.settle()
                chain.did(apart(ve_.copy_predicated(cur[:, :], above[:, :, :], prev[:, :])))
                chain.settle()
                wait(dve, probs_made, step - 1)
                chain.did(ve_.tensor_reduce(mx[:, s % 2, :], cur[:, :].rearrange("p (h c) -> p h c", h=4), AX.X, ALU.max))
                chain.settle()
                ve_.tensor_scalar(nmx[:, s % 2, :], mx[:, s % 2, :], -SCALE, None, ALU.mult).then_inc(nmx_made, 1)

            def keep_keys(i, h, s):
                step = (i * 2 + h) * 8 + s
                wait(dve, pT_done, step + 1)
                wait(dve, pv_done, step - 1)
                ve_.tensor_tensor(pT_cur[:, s % 2, :], pT_ps[:, :], keep_cur[:, :], ALU.mult)
                ve_.tensor_tensor(pT_prev[:, s % 2, :], pT_ps[:, :], keep_prev[:, :], ALU.mult).then_inc(pT_made, 1)

            def normalise(n, a):
                wait(dve, pv_done, n * 4 + 4)
                wait(dve, oT_tr, n * 2)
                ve_.reciprocal(rsum[:, :], psum_row[:, a, :]).then_inc(rsum_made, 1)
                wait(dve, rsum_made, n + 1)
                ve_.tensor_tensor(o_sb[:, :].rearrange("p (h d) -> p h d", h=H), o_ps[:, :].rearrange("p (h d) -> p h d", h=H),
                                  rsum[:, :].unsqueeze(2).to_broadcast([P, H, DH]), ALU.mult).then_inc(o_made, 1)

            def combine(n, a, slot, i):
                k = i
                wait(dve, acc_in[slot], k * 16 + 16)
                rounds = k * 2 + (slot // 2) + 1
                wait(dve, y1_in[a], rounds * 16)
                wait(dve, y2_in[a], rounds * 16)
                ve_.scalar_tensor_tensor(acc[:, slot, :], y1[:, a, :], w1[:, bass.ds(n, 1)], acc[:, slot, :], ALU.mult, ALU.add).then_inc(comb_step, 1)
                wait(dve, comb_step, n * 2 + 1)
                ve_.scalar_tensor_tensor(acc[:, slot, :], y2[:, a, :], w2[:, bass.ds(n, 1)], acc[:, slot, :], ALU.mult, ALU.add).then_inc(comb_step, 1)

            for u, unit in enumerate(PROJECTION):
                read_unit(unit, u, -1)
            chain = Chain(dve, merge_step, 0)
            merge(0, 0, 0, chain)
            FIRST = chain.n

            def body(i):
                chain = Chain(dve, merge_step, i * MERGE + FIRST)
                for h in range(2):
                    h_now[0] = h
                    pair, u = i * 2 + h, 0
                    for s in range(8):
                        if not (is_last(i, NB) and h == 1 and s == 7):
                            merge(i, h, s + 1, chain)
                        keep_keys(i, h, s)
                        if s == 0 and not (is_first(i) and h == 0):
                            normalise(pair * 2 - 1, 1)
                        if s == 4:
                            normalise(pair * 2, 0)
                        if s == 3 and not (is_first(i) and h == 0):
                            combine(pair * 2 - 1, 1, (2 * h - 1) % 4, i if h else i - 1)
                        if s == 5:
                            combine(pair * 2, 0, 2 * h, i)
                        for unit in SCHEDULE[s]:
                            if unit_exists(unit, i, h):
                                if unit[0] == "wo":
                                    wait(dve, comb_step, (pair * 2 - (1 if unit[1] else 0)) * 2 + 2)
                                read_unit(unit, u, pair)
                            u += 1
                if not is_last(i, NB):
                    assert chain.n == MERGE, chain.n

            repeated(dve, NB, body)
            h_now[0] = 0
            normalise(NT - 1, 1)
            combine(NT - 1, 1, 3, NB - 1)
            for unit in (("oT", 1, 0), ("oT", 1, 1), ("wo", 1, 0), ("wo", 1, 1)):
                if unit[0] == "wo":
                    wait(dve, comb_step, NT * 2)
                read_unit(unit, unit[2], NP)


_INS = ["L0_attn_x", "L0_attn_g", "L0_attn_Wqkv", "L0_attn_Wo", "L0_ffn_wg", "L0_ffn_we"]


def kernel(**inputs):
    import numpy as np
    from concourse import bacc
    from concourse.bass_utils import run_bass_kernel_spmd

    nc = bacc.Bacc("TRN2", target_bir_lowering=False, num_devices=1)
    arrays, args = {}, []
    for name in _INS:
        a = np.ascontiguousarray(inputs[name])
        arrays[f"in_{name}"] = a
        args.append(nc.dram_tensor(f"in_{name}", a.shape, mybir.dt.from_np(a.dtype), kind="ExternalInput").ap())
    out = nc.dram_tensor("out", arrays["in_L0_attn_x"].shape, F32, kind="ExternalOutput").ap()
    telephone_moe(nc, *args, out)
    r = run_bass_kernel_spmd(nc, [arrays], core_ids=[0])
    return r.results[0]["out"]
```

```python
from contextlib import ExitStack

import concourse.bass as bass
from concourse import mybir

F32 = mybir.dt.float32
F32R = mybir.dt.float32r
BF16 = mybir.dt.bfloat16
I32 = mybir.dt.int32
U32 = mybir.dt.uint32
I8 = mybir.dt.int8
ALU = mybir.AluOpType
ACT = mybir.ActivationFunctionType
AX = mybir.AxisListType

P = 128
NUM_HEADS = 16
LN_EPS = 1e-5
RMS_EPS = 1e-6
GATE_EPS = 1.1920929e-07
MASKED = -3.0e38


def wait(eng, sem, value):
    if isinstance(value, int) and value <= 0:
        return
    eng.wait_ge(sem, value)


class Chain:

    def __init__(self, eng, sem, base):
        self.eng, self.sem, self.base, self.n = eng, sem, base, 0

    def did(self, ins):
        ins.then_inc(self.sem, 1)
        self.n += 1

    def settle(self):
        self.eng.wait_ge(self.sem, self.base + self.n)


def repeated(eng, count, body):
    body(0)
    with eng.Fori(1, count - 1) as i:
        body(i)
    body(count - 1)


def is_last(i, count):
    return isinstance(i, int) and i == count - 1


def is_first(i):
    return isinstance(i, int) and i == 0


def telephone_moe(nc, x, g, wqkv, wo, wg, we, out):
    B, S, D = x.shape
    T = B * S
    E = wg.shape[1]
    CAP = P
    KT = D // P
    H, DH = NUM_HEADS, D // NUM_HEADS
    SCALE = float(DH) ** -0.5
    NT = T // P
    TB = 4
    NB = NT // TB
    EB = 4
    NE = E // EB
    NP = NT // 2
    GRP = H // 4
    PER_SEQ = S // P // TB
    assert D == 512 and E == 128 and DH == 32 and CAP == 128

    x_rows = x.rearrange("b s d -> (b s) d")
    out_rows = out.rearrange("b s d -> (b s) d")
    xa_rows = nc.dram_tensor("xa_rows", [T, D], F32, kind="Internal")
    xpx_rows = nc.dram_tensor("xpx_rows", [T, D], F32, kind="Internal")
    yb_rows = nc.dram_tensor("yb_rows", [E * CAP, D], F32, kind="Internal")

    ctx = ExitStack()
    early = ExitStack()
    with ctx:
        def sb(name, shape, dt=F32, where=ctx):
            return where.enter_context(nc.sbuf_tensor(name, shape, dt))

        def sem(name):
            return ctx.enter_context(nc.semaphore(name))

        def sems(name, n):
            return [sem(f"{name}{k}") for k in range(n)]

        wqkv_hi = sb("wqkv_hi", [P, KT, 3 * D], F32R)
        wqkv_lo = sb("wqkv_lo", [P, KT, 3 * D], F32R)
        wo_hi = sb("wo_hi", [P, KT, D], F32R)
        wo_lo = sb("wo_lo", [P, KT, D], F32R)
        ident = sb("ident", [P, P])
        above = sb("above", [P, 4, P], I8)
        keep_prev = sb("keep_prev", [P, 4 * P], BF16)
        prev_cap = sb("prev_cap", [P, NB])
        slot1 = sb("slot1", [P, NT], I32)
        slot2 = sb("slot2", [P, NT], I32)
        w1 = sb("w1", [P, NT])
        w2 = sb("w2", [P, NT])

        def early_sb(name, shape, dt=F32):
            return sb(name, shape, dt, early)

        tri = early_sb("tri", [P, P], BF16)
        ones = early_sb("ones", [P, P], BF16)
        zeros = early_sb("zeros", [P, 2 * P], BF16)
        iota_row = early_sb("iota_row", [P, P])
        lane_tile = early_sb("lane_tile", [P, NT, 2])
        mask2_all = early_sb("mask2_all", [P, NT, E], BF16)
        gvec = early_sb("gvec", [P, KT])
        wgate = early_sb("wgate", [P, KT, E])
        x1 = early_sb("x1", [P, TB, D])
        xa1 = early_sb("xa1", [P, TB, D])
        xp1 = early_sb("xp1", [P, TB, D])
        xT1 = early_sb("xT1", [P, 2, KT, P])
        bn6 = early_sb("bn6", [P, TB, 6])
        mv = early_sb("mv", [P, TB, 2])
        ve = early_sb("ve", [P, TB])
        root = early_sb("root", [P, TB])
        rstd = early_sb("rstd", [P, TB])
        r2 = early_sb("r2", [P, TB])
        tmp4 = early_sb("tmp4", [P, TB])
        ms = early_sb("ms", [P, TB])
        comb = early_sb("comb", [P, TB])
        ir2 = early_sb("ir2", [P, NT])
        logit_all = early_sb("logit_all", [P, NT, E])
        top8 = early_sb("top8", [P, TB, 8])
        idx8 = early_sb("idx8", [P, TB, 8], U32)
        e12 = early_sb("e12", [P, 2, TB])
        l1 = early_sb("l1", [P, NT])
        l2 = early_sb("l2", [P, NT])
        e1 = early_sb("e1", [P, NT])
        e2 = early_sb("e2", [P, NT])
        loc1 = early_sb("loc1", [P, NT])
        rank2 = early_sb("rank2", [P, NT])
        base2 = early_sb("base2", [P, NT])
        loc2 = early_sb("loc2", [P, NT])
        loc4 = early_sb("loc4", [P, 2, TB])
        logit_now = early_sb("logit_now", [P, TB, E])
        mask = early_sb("mask", [P, TB, 2 * E], BF16)
        before = early_sb("before", [P, TB, 2 * E], BF16)
        place = early_sb("place", [P, TB, 2 * CAP], BF16)
        junk = early_sb("junk", [P, 4, P])
        junk2 = early_sb("junk2", [P, 4, P])
        nbias = early_sb("nbias", [P, TB])
        rplus = early_sb("rplus", [P, TB])
        nbias_x = early_sb("nbias_x", [P, TB])
        junk_z = early_sb("junk_z", [P, 2, P])
        count1 = early_sb("count1", [P, E])
        ids_hi = early_sb("ids_hi", [P, CAP])
        ids = early_sb("ids", [P, CAP])
        idx_all = early_sb("idx_all", [P, E], I32)
        zsum = early_sb("zsum", [P, NT])
        nmax = early_sb("nmax", [P, NT])
        ga = early_sb("ga", [P, NT])
        gb = early_sb("gb", [P, NT])
        gc = early_sb("gc", [P, NT])
        wexp = early_sb("wexp", [P, EB, KT, D])
        idx_now = early_sb("idx_now", [P, EB], I32)
        rows = early_sb("rows", [P, EB, D])
        rowsT, ysb = xT1, x1
        raw = [rows[:, :, :].rearrange("p b d -> p (b d)"), wexp[:, EB - 1, :, :].rearrange("p k d -> p (k d)")]
        early.close()

        q_stack = sb("q_stack", [P, 2, H, 2 * P], F32R)
        k_stack = sb("k_stack", [P, 2, H, 2 * P], F32R)
        kq_hi = sb("kq_hi", [P, 2, GRP, 2 * P], F32R)
        kq_lo = sb("kq_lo", [P, 2, GRP, 2 * P], F32R)
        xT_hi = sb("xT_hi", [P, KT, 2 * P], F32R)
        xT_lo = sb("xT_lo", [P, KT, 2 * P], F32R)
        v_sb = sb("v_sb", [P, 4, D])
        v_change = sb("v_change", [P, 2, D])
        xa3 = sb("xa3", [P, 2, 2, D])
        acc = sb("acc", [P, 4, D])
        y1 = sb("y1", [P, 2, D])
        y2 = sb("y2", [P, 2, D])
        probs = sb("probs", [P, 2, 4 * P])
        pT_all = sb("pT_all", [P, 2, 4 * P])
        pT_prev = sb("pT_prev", [P, 2, 4 * P])
        oT_hi = sb("oT_hi", [P, KT, P], F32R)
        oT_lo = sb("oT_lo", [P, KT, P], F32R)
        mx = sb("mx", [P, 2, 4])
        nmx = sb("nmx", [P, 2, 4])
        psum_row = sb("psum_row", [P, 2, 4])
        rsum = sb("rsum", [P, 2, 4])
        slot_now = sb("slot_now", [P, 2, 2], I32)

        banks = [ctx.enter_context(nc.psum_tensor(f"bank{k}", [P, 512], F32)) for k in range(8)]
        t_ps, logit_ps, pos_ps, table_ps, y_ps = banks[0:2], banks[2:4], banks[4:6], banks[6], banks[2:4]
        score_ps = [[banks[0], banks[1]], [banks[2], banks[3]]]
        pT_ps, o_ps, unit_ps = banks[4], banks[5], banks[6:8]

        const_made = sem("const_made")
        gvec_in, wgate_in, raw_in = sem("gvec_in"), sem("wgate_in"), sems("raw_in", 2)
        weights_split, raw_scaled, raw_rounded = sem("weights_split"), sem("raw_scaled"), sem("raw_rounded")
        x_in = sems("x_in", TB)
        stat_step, route_step, late_step = sem("stat_step"), sem("route_step"), sem("late_step")
        root_wanted, root_made = sem("root_wanted"), sem("root_made")
        factors_made, xa_made, xpx_made = sem("factors_made"), sem("xa_made"), sem("xpx_made")
        xa_out, xpx_out = sems("xa_out", TB), sems("xpx_out", TB)
        t_done, xT_made = sem("t_done"), sem("xT_made")
        logits_done, logits_kept, logits_ranked = sem("logits_done"), sem("logits_kept"), sem("logits_ranked")
        mask_made, pos_done, pos_read = sem("mask_made"), sem("pos_done"), sem("pos_read")
        place_made, table_done = sem("place_made"), sem("table_done")
        mask2_kept, base_step = sem("mask2_kept"), sem("base_step")
        count_done, place2_made, table2_done = sem("count_done"), sem("place2_made"), sem("table2_done")
        ids_made, idsT_done, idx_made = sem("ids_made"), sem("idsT_done"), sem("idx_made")
        nmax_made, z_made, gate_exp = sem("nmax_made"), sem("z_made"), sem("gate_exp")
        wexp_in, rows_in, ysb_out = sems("wexp_in", EB), sems("rows_in", EB), sems("ysb_out", EB)
        idx_copied, rowsT_done, rowsT_made = sem("idx_copied"), sem("rowsT_done"), sem("rowsT_made")
        y_done, y_copied, routing_made = sem("y_done"), sem("y_copied"), sem("routing_made")
        xa3_in, acc_in, acc_out = sems("xa3_in", 2), sems("acc_in", 4), sems("acc_out", 4)
        y1_in, y2_in, slot_copied = sems("y1_in", 2), sems("y2_in", 2), sem("slot_copied")
        init3 = sem("init3")
        xT_tr, xT_hi_made, xT_split = sem("xT_tr"), sem("xT_hi_made"), sem("xT_split")
        kq_done, kq_hi_made, kq_split = sem("kq_done"), sem("kq_hi_made"), sem("kq_split")
        k_stacked, q_stacked = sem("k_stacked"), sem("q_stacked")
        v_done, v_made = sem("v_done"), sem("v_made")
        score_done, merge_step, nmx_made = sem("score_done"), sem("merge_step"), sem("nmx_made")
        probs_made, pT_done, pT_made = sem("probs_made"), sem("pT_done"), sem("pT_made")
        pT_copied, v_changed = sem("pT_copied"), sem("v_changed")
        rsum_made, probs_scaled, pv_done = sem("rsum_made"), sem("probs_scaled"), sem("pv_done")
        oT_hi_made, oT_split = sem("oT_hi_made"), sem("oT_split")
        h_done, comb_step, fin_done = sem("h_done"), sem("comb_step"), sem("fin_done")

        block = ctx.enter_context(nc.Block())

        def strided(ap, k):
            return ap.rearrange("p (c k) -> p k c", k=KT)[:, k, :]

        CONSTS = 11
        STACKED, STACK_DMAS = 3, 12
        KP = STACKED * DH

        def apart(ins):
            return ins.wait_op(const_made, CONSTS, "sem-ge")

        def experts_done(eng):
            eng.wait_ge(routing_made, 1)
            for b in range(EB):
                eng.wait_ge(ysb_out[b], 16 * NE)

        @block.sync
        def _(sp):
            def load_x(n, j):
                sp.dma_start(x1[:, j, :], x_rows[bass.ds(n * P, P), :]).then_inc(x_in[j], 16)

            for j in range(TB):
                load_x(j, j)
            sp.dma_start(wgate[:, :, :], wg.rearrange("(p k) e -> p k e", k=KT)).then_inc(wgate_in, 16)
            sp.dma_start(gvec[:, :], g.rearrange("(p k) -> p k", k=KT)).then_inc(gvec_in, 16)

            def load_expert(e, b):
                sp.dma_start(wexp[:, b, :, :], we[bass.ds(e, 1), :, :].rearrange("e (p k) f -> p (e k) f", k=KT)).then_inc(wexp_in[b], 16)

            for b in range(EB - 1):
                load_expert(b, b)

            def norm_body(i):
                for j in range(TB):
                    n = i * TB + j
                    wait(sp, xa_made, n + 1)
                    sp.dma_start(xa_rows[bass.ds(n * P, P), :], xa1[:, j, :]).then_inc(xa_out[j], 16)
                    wait(sp, xpx_made, n + 1)
                    sp.dma_start(xpx_rows[bass.ds(n * P, P), :], xp1[:, j, :]).then_inc(xpx_out[j], 16)
                    if not is_last(i, NB):
                        load_x(n + TB, j)

            repeated(sp, NB, norm_body)
            sp.wait_ge(weights_split, KT + 1)
            load_expert(EB - 1, EB - 1)

            def expert_loads(i):
                for b in range(EB):
                    n = i * EB + b
                    wait(sp, y_done, n + 1)
                    load_expert(n + EB, b)

            with sp.Fori(0, NE - 1) as i:
                expert_loads(i)

            experts_done(sp)

            def load_xa3(pair, h):
                sp.dma_start(xa3[:, h, :, :], xa_rows[bass.ds(pair * 2 * P, 2 * P), :].rearrange("(a p) d -> p a d", p=P)).then_inc(xa3_in[h], 16)

            def load_acc(n, slot):
                sp.dma_start(acc[:, slot, :], xpx_rows[bass.ds(n * P, P), :]).then_inc(acc_in[slot], 16)

            def stack(dst, src, done, h):
                for r in range(STACKED):
                    for q in range(4):
                        sp.dma_start(dst[32 * r:32 * r + 32, h, 4 * q:4 * q + 4, :].bitcast(F32),
                                     src[r][32 * q:32 * q + 32, :, :].bitcast(F32)).then_inc(done, 16)

            K_PARTS = [kq_hi[:, 0], kq_lo[:, 0], kq_hi[:, 0]]
            Q_PARTS = [kq_hi[:, 1], kq_hi[:, 1], kq_lo[:, 1]]

            def stack_pair(pair, h):
                wait(sp, kq_split, pair * 8 + 4)
                wait(sp, score_done, (pair - 1) * 8 + 4)
                stack(k_stack, K_PARTS, k_stacked, h)
                wait(sp, kq_split, pair * 8 + 8)
                stack(q_stack, Q_PARTS, q_stacked, h)

            def store(n, slot):
                wait(sp, fin_done, n * 2 + 2)
                sp.dma_start(out_rows[bass.ds(n * P, P), :], acc[:, slot, :]).then_inc(acc_out[slot], 16)

            load_xa3(0, 0)
            load_xa3(1, 1)
            load_acc(0, 0)
            sp.wait_ge(init3, 2)
            stack_pair(0, 0)

            def pair_body(i, h):
                pair = i * 2 + h
                last = is_last(i, NB)
                if not last:
                    wait(sp, xT_tr, pair * 2 + 2)
                    load_xa3(pair + 2, h)
                for n, slot in ((pair * 2 + 1, (2 * h + 1) % 4), (pair * 2 + 2, (2 * h + 2) % 4)):
                    if last and h == 1 and slot == 0:
                        continue
                    k = i if slot > 2 * h else i + 1
                    wait(sp, acc_out[slot], k * 16)
                    load_acc(n, slot)
                if not (last and h == 1):
                    stack_pair(pair + 1, 1 - h)
                if not (is_first(i) and h == 0):
                    store(pair * 2 - 1, (2 * h - 1) % 4)
                store(pair * 2, 2 * h)

            def body(i):
                for h in range(2):
                    pair_body(i, h)

            repeated(sp, NB, body)
            store(NT - 1, 3)
            for k in range(4):
                sp.wait_ge(acc_out[k], 16 * NB)

        @block.gpsimd
        def _(pool):
            gp = nc.gpsimd
            gp.memset(ident[:, :], 0.0).then_inc(const_made, 1)
            gp.memset(tri[:, :], 1.0).then_inc(const_made, 1)
            gp.memset(ones[:, :], 1.0).then_inc(const_made, 1)
            gp.memset(zeros[:, :], 0.0).then_inc(const_made, 1)
            gp.memset(keep_prev[:, :], 1.0).then_inc(const_made, 1)
            gp.iota(iota_row[:, :], [[1, P]], base=0, channel_multiplier=0, allow_small_or_imprecise_dtypes=True).then_inc(const_made, 1)
            gp.iota(lane_tile[:, :, 1], [[1, NT]], base=0, channel_multiplier=0, allow_small_or_imprecise_dtypes=True).then_inc(const_made, 1)
            gp.iota(lane_tile[:, :, 0], [[0, NT]], base=0, channel_multiplier=1, allow_small_or_imprecise_dtypes=True).then_inc(const_made, 1)
            gp.memset(prev_cap[:, :], -MASKED).then_inc(const_made, 1)
            gp.memset(above[:, :, :], 1).then_inc(const_made, 1)
            gp.memset(before[:, 0, :], 0.0).then_inc(const_made, 1)
            pool.wait_ge(const_made, CONSTS)
            gp.affine_select(out=ident[:, :], in_=ident[:, :], compare_op=ALU.not_equal, fill=1.0, base=0,
                             pattern=[[-1, P]], channel_multiplier=1).then_inc(const_made, 1)
            gp.affine_select(out=tri[:, :], in_=tri[:, :], compare_op=ALU.is_gt, fill=0.0, base=0,
                             pattern=[[1, P]], channel_multiplier=-1).then_inc(const_made, 1)
            gp.affine_select(out=keep_prev[:, :], in_=keep_prev[:, :], compare_op=ALU.is_gt, fill=0.0, base=0,
                             pattern=[[0, 4], [-1, P]], channel_multiplier=1).then_inc(const_made, 1)
            gp.affine_select(out=above[:, :, :], in_=above[:, :, :], compare_op=ALU.is_gt, fill=0.0, base=0,
                             pattern=[[0, 4], [1, P]], channel_multiplier=-1).then_inc(const_made, 1)
            for b in range(B):
                gp.memset(prev_cap[:, b * PER_SEQ:b * PER_SEQ + 1], MASKED).then_inc(const_made, 1)

            def load_raw(c):
                if c < KT:
                    pool.dma_start(raw[c % 2][:, 0:3 * D], wqkv.rearrange("(p k) n -> p k n", k=KT)[:, c, :]).then_inc(raw_in[c % 2], 16)
                else:
                    pool.dma_start(raw[c % 2].rearrange("p (k n) -> p k n", k=KT), wo.rearrange("(k p) n -> p k n", p=P)).then_inc(raw_in[c % 2], 16)

            def split_raw(c):
                pool.wait_ge(raw_in[c % 2], 16 * (c // 2 + 1))
                if c < KT:
                    part, hi, lo = raw[c % 2][:, 0:3 * D], wqkv_hi[:, c, :], wqkv_lo[:, c, :]
                    gp.tensor_scalar(part, part, gvec[:, c:c + 1], None, ALU.mult).then_inc(raw_scaled, 1)
                    pool.wait_ge(raw_scaled, c + 1)
                else:
                    part, hi, lo = raw[c % 2], wo_hi[:, :, :].rearrange("p k n -> p (k n)"), wo_lo[:, :, :].rearrange("p k n -> p (k n)")
                gp.tensor_copy(hi, part).then_inc(raw_rounded, 1)
                pool.wait_ge(raw_rounded, c + 1)
                gp.tensor_tensor(lo, part, hi.bitcast(F32), ALU.subtract).then_inc(weights_split, 1)
                pool.wait_ge(weights_split, c + 1)

            pool.wait_ge(gvec_in, 16)
            load_raw(0)
            load_raw(1)

            def norm_body(i):
                wait(pool, factors_made, i + 1)
                for j in range(TB):
                    wait(pool, xpx_out[j], i * 16)
                    apart(gp.tensor_scalar(xp1[:, j, :], x1[:, j, :], rplus[:, j:j + 1], nbias_x[:, j:j + 1],
                                           ALU.mult, ALU.add)).then_inc(xpx_made, 1)

            def keep_masks(i):
                for j in range(TB):
                    n = i * TB + j
                    wait(pool, mask_made, n + 1)
                    gp.tensor_copy(mask2_all[:, bass.ds(n, 1), :], mask[:, j, E:2 * E]).then_inc(mask2_kept, 1)

            def split_and_load(c):
                split_raw(c)
                if c + 2 <= KT:
                    load_raw(c + 2)

            norm_body(0)

            def keep_body(i):
                if not is_last(i, NB):
                    norm_body(i + 1)
                keep_masks(i)

            EARLY_CHUNKS = 3
            for c in range(EARLY_CHUNKS):
                keep_body(c)
                split_and_load(c)
            with pool.Fori(EARLY_CHUNKS, NB - 1) as i:
                keep_body(i)
            keep_body(NB - 1)
            for c in range(EARLY_CHUNKS, KT + 1):
                split_and_load(c)

            for j in range(TB):
                pool.wait_ge(xa_out[j], 16 * NB)
            pool.wait_ge(idx_made, 1)

            def expert_body(i):
                for b in range(EB):
                    n = i * EB + b
                    wait(pool, rows_in[b], i * 16)
                    wait(pool, rowsT_done, n + 1 - EB)
                    gp.tensor_copy(idx_now[:, b:b + 1], idx_all[:, bass.ds(n, 1)]).then_inc(idx_copied, 1)
                    wait(pool, idx_copied, n + 1)
                    apart(gp.indirect_dma_start(rows[:, b, :], None, xa_rows[:, :],
                                          bass.IndirectOffsetOnAxis(ap=idx_now[:, b:b + 1], axis=0))).then_inc(rows_in[b], 16)

            repeated(pool, NE, expert_body)

            experts_done(pool)
            gp.memset(v_sb[:, 3, :], 0.0).then_inc(init3, 1)
            gp.memset(k_stack[:, 1, :, :].bitcast(F32), 0.0).then_inc(init3, 1)

            def scale_probs(step, s):
                wait(pool, rsum_made, step + 1)
                part = probs[:, s % 2, :].rearrange("p (h c) -> p h c", h=4)
                gp.tensor_tensor(part, part, rsum[:, s % 2, :].unsqueeze(2).to_broadcast([P, 4, P]), ALU.mult).then_inc(probs_scaled, 1)

            def mask_probs(step, s):
                wait(pool, pT_copied, step + 1)
                gp.tensor_tensor(pT_prev[:, s % 2, :], pT_all[:, s % 2, :], keep_prev[:, :], ALU.mult).then_inc(pT_made, 1)

            def change_values(n, j):
                wait(pool, v_made, n * 2 + 2)
                wait(pool, pv_done, n * 4 - 4)
                gp.tensor_tensor(v_change[:, j % 2, :], v_sb[:, (j - 1) % 4, :], v_sb[:, j, :], ALU.subtract).then_inc(v_changed, 1)

            scale_probs(0, 0)
            change_values(0, 0)

            def gather_body(i):
                for j in range(TB):
                    n, a = i * TB + j, j % 2
                    wait(pool, comb_step, (n - 1) * 2)
                    gp.tensor_copy(slot_now[:, a, 0:1], slot1[:, bass.ds(n, 1)]).then_inc(slot_copied, 1)
                    gp.tensor_copy(slot_now[:, a, 1:2], slot2[:, bass.ds(n, 1)]).then_inc(slot_copied, 1)
                    wait(pool, slot_copied, n * 2 + 2)
                    apart(gp.indirect_dma_start(y1[:, a, :], None, yb_rows[:, :],
                                          bass.IndirectOffsetOnAxis(ap=slot_now[:, a, 0:1], axis=0))).then_inc(y1_in[a], 16)
                    apart(gp.indirect_dma_start(y2[:, a, :], None, yb_rows[:, :],
                                          bass.IndirectOffsetOnAxis(ap=slot_now[:, a, 1:2], axis=0))).then_inc(y2_in[a], 16)
                    for grp in range(4):
                        if not (is_last(i, NB) and j == TB - 1 and grp == 3):
                            scale_probs(n * 4 + grp + 1, grp + 1)
                        mask_probs(n * 4 + grp, grp)
                        if grp == 1 + a and not (is_last(i, NB) and j == TB - 1):
                            change_values(n + 1, (j + 1) % TB)

            repeated(pool, NB, gather_body)

        SCHEDULE = [
            [("kq", 0, 0), ("kq", 0, 1)],
            [("kq", 0, 2), ("kq", 0, 3)],
            [("kq", 1, 0), ("kq", 1, 1), ("kq", 1, 2)],
            [("kq", 1, 3), ("wo", 1, 0)],
            [("wo", 1, 1), ("v", 0, 0)],
            [("v", 0, 1), ("wo", 0, 0)],
            [("wo", 0, 1), ("v", 1, 0)],
            [("xT", 0, 0), ("v", 1, 1), ("xT", 1, 0)],
        ]
        AHEAD = [0, 0, 0, 0, 1, 0, 0, 0]
        READ_EARLY = [1, 1, 1, 1, 0, 0, 0, 2]
        UNITS = [u for step in SCHEDULE for u in step]
        PROJECTION = ([(u, -2) for u in UNITS if u[0] == "xT"] + [(u, -1) for u in UNITS if u[0] in ("kq", "v")]
                      + [(u, -1) for u in UNITS if u[0] == "xT"])
        assert len(UNITS) == 18

        def unit_exists(unit, i, h):
            kind, a, _ = unit
            if kind == "xT":
                return not is_last(i, NB)
            if kind in ("kq", "v"):
                return not (is_last(i, NB) and h == 1)
            return not (a == 1 and is_first(i) and h == 0)

        def unit_index(unit, pair):
            kind, a, c = unit
            if kind == "xT":
                return pair * 2 + 4 + a
            if kind == "v":
                return pair * 4 + 4 + 2 * a + c
            if kind == "kq":
                return pair * 8 + 8 + 4 * a + c
            n = pair * 2 - 1 if a == 1 else pair * 2
            return n * 2 + c

        CONSUMED = {"xT": xT_split, "kq": kq_split, "v": v_made, "wo": fin_done}

        @block.tensor
        def _(pe):
            mm = nc.tensor.matmul

            pe.wait_ge(const_made, CONSTS + 4)
            pe.wait_ge(wgate_in, 16)
            mm(table_ps[:, 0:2 * CAP], zeros[:, 0:P], zeros[:, :], start=True, stop=True)

            def transposes(i, j):
                n = i * TB + j
                wait(pe, xa_made, n + 1)
                wait(pe, xT_made, n - 1)
                for k in range(KT):
                    ins = nc.tensor.transpose(t_ps[j % 2][:, k * P:(k + 1) * P], strided(xa1[:, j, :], k), ident[:, :])
                ins.then_inc(t_done, 1)

            def logits(i, j):
                n = i * TB + j
                wait(pe, xT_made, n + 1)
                wait(pe, logits_kept, n - 1)
                for k in range(KT):
                    ins = mm(logit_ps[j % 2][:, 0:E], xT1[:, j % 2, k, :], wgate[:, k, :], start=(k == 0), stop=(k == KT - 1))
                ins.then_inc(logits_done, 1)

            def positions(i, j):
                n = i * TB + j
                wait(pe, mask_made, n + 1)
                wait(pe, pos_read, n - 1)
                mm(pos_ps[j % 2][:, 0:2 * E], tri[:, :], mask[:, j, :], start=True, stop=False)
                mm(pos_ps[j % 2][:, 0:2 * E], ones[:, :], before[:, j, :], start=False, stop=True).then_inc(pos_done, 1)

            def table(sem_ready, sem_done, experts, i, j):
                wait(pe, sem_ready, i * TB + j + 1)
                mm(table_ps[:, 0:2 * CAP], experts, place[:, j, :], start=False, stop=True, skip_group_check=True).then_inc(sem_done, 1)

            def front(i, between):
                transposes(i, 0)
                transposes(i, 1)
                logits(i, 0)
                between(0)
                transposes(i, 2)
                between(1)
                logits(i, 1)
                between(2)
                transposes(i, 3)
                between(3)
                logits(i, 2)
                logits(i, 3)

            front(0, lambda j: None)

            def norm_body(i):
                if is_last(i, NB):
                    for j in range(TB):
                        positions(i, j)
                else:
                    front(i + 1, lambda j: positions(i, j))
                for j in range(TB):
                    table(place_made, table_done, mask[:, j, 0:E], i, j)

            repeated(pe, NB, norm_body)
            mm(pos_ps[0][:, 0:2 * E], ones[:, :], before[:, 0, :], start=True, stop=True).then_inc(count_done, 1)

            def second_body(i):
                for j in range(TB):
                    table(place2_made, table2_done, mask2_all[:, bass.ds(i * TB + j, 1), :].rearrange("p a e -> p (a e)"), i, j)

            pe.wait_ge(mask2_kept, NT)
            repeated(pe, NB, second_body)
            pe.wait_ge(ids_made, 1)
            nc.tensor.transpose(pos_ps[1][:, 0:P], ids[:, :], ident[:, :]).then_inc(idsT_done, 1)

            def rows_transposed(n, b, i):
                wait(pe, rows_in[b], i * 16 + 16)
                wait(pe, rowsT_made, n - 1)
                for k in range(KT):
                    ins = nc.tensor.transpose(t_ps[b % 2][:, k * P:(k + 1) * P], strided(rows[:, b, :], k), ident[:, :])
                ins.then_inc(rowsT_done, 1)

            def expert_product(n, b, i):
                wait(pe, rowsT_made, n + 1)
                wait(pe, wexp_in[b], i * 16 + 16)
                wait(pe, y_copied, n - 1)
                for k in range(KT):
                    ins = mm(y_ps[b % 2][:, :], rowsT[:, b % 2, k, :], wexp[:, b, k, :], start=(k == 0), stop=(k == KT - 1))
                ins.then_inc(y_done, 1)

            rows_transposed(0, 0, 0)

            def expert_body(i):
                for b in range(EB):
                    n = i * EB + b
                    if not (is_last(i, NE) and b == EB - 1):
                        rows_transposed(n + 1, (b + 1) % EB, i + (b + 1) // EB)
                    expert_product(n, b, i)

            repeated(pe, NE, expert_body)

            experts_done(pe)
            pe.wait_ge(weights_split, KT + 1)

            def half(u):
                return unit_ps[u % 2][:, 0:256]

            def split_product(dst, left_hi, left_lo, right_hi, right_lo, done):
                for k in range(KT):
                    for p, (a, b) in enumerate(((left_hi, right_hi), (left_hi, right_lo), (left_lo, right_hi))):
                        ins = mm(dst, a(k), b(k), start=(k == 0 and p == 0), stop=(k == KT - 1 and p == 2))
                ins.then_inc(done, 1)

            def run_unit(unit, u, pair, h):
                kind, a, c = unit
                n = pair * 2 - 1 if a == 1 else pair * 2
                dst = half(u)
                if kind == "xT":
                    if a == 0:
                        wait(pe, xa3_in[h], (body_of[0] + 2) * 16)
                    for k in range(KT):
                        ins = nc.tensor.transpose(unit_ps[u % 2][:, k * P:(k + 1) * P], strided(xa3[:, h, a, :], k), ident[:, :])
                    ins.then_inc(xT_tr, 1)
                elif kind == "kq":
                    if (a, c) == (0, 0):
                        wait(pe, xT_split, pair * 2 + 4)
                    col = (D if a == 0 else 0) + c * P
                    split_product(dst, lambda k: wqkv_hi[:, k, col:col + P], lambda k: wqkv_lo[:, k, col:col + P],
                                  lambda k: xT_hi[:, k, :], lambda k: xT_lo[:, k, :], kq_done)
                elif kind == "v":
                    col = 2 * D + c * 256
                    split_product(dst, lambda k: xT_hi[:, k, a * P:(a + 1) * P], lambda k: xT_lo[:, k, a * P:(a + 1) * P],
                                  lambda k: wqkv_hi[:, k, col:col + 256], lambda k: wqkv_lo[:, k, col:col + 256], v_done)
                else:
                    wait(pe, oT_split, n + 1)
                    col = c * 256
                    split_product(dst, lambda k: oT_hi[:, k, :], lambda k: oT_lo[:, k, :],
                                  lambda k: wo_hi[:, k, col:col + 256], lambda k: wo_lo[:, k, col:col + 256], h_done)

            body_of = [0]

            def scores(i, h, s):
                if s >= 8:
                    i, h, s = (i, 1, s - 8) if h == 0 else (i + 1, 0, s - 8)
                pair = i * 2 + h
                step, a, grp = pair * 8 + s, s // 4, s % 4
                if s == 0:
                    wait(pe, k_stacked, (pair + 1) * STACK_DMAS * 16)
                    wait(pe, q_stacked, (pair + 1) * STACK_DMAS * 16)
                wait(pe, probs_made, step - 1)
                dst_prev, dst_cur = score_ps[s % 2]
                for hh in range(4):
                    place = hh * 4 + grp
                    q_part = q_stack[0:KP, h, place, a * P:(a + 1) * P]
                    k_prev = k_stack[0:KP, h, place, 0:P] if a == 1 else k_stack[0:KP, 1 - h, place, P:2 * P]
                    mm(dst_cur[:, hh * P:(hh + 1) * P], q_part, k_stack[0:KP, h, place, a * P:(a + 1) * P], start=True, stop=True)
                    ins = mm(dst_prev[:, hh * P:(hh + 1) * P], q_part, k_prev, start=True, stop=True)
                ins.then_inc(score_done, 1)

            def values(i, h, s):
                if s == -1:
                    if is_first(i) and h == 0:
                        return
                    i, h, s = (i, 0, 7) if h == 1 else (i - 1, 1, 7)
                step, a, grp = (i * 2 + h) * 8 + s, s // 4, s % 4
                n = (i * 2 + h) * 2 + a
                slot = 2 * h + a
                wait(pe, pT_made, step + 1)
                if grp == 0:
                    wait(pe, v_changed, n + 1)
                    wait(pe, oT_split, n)
                for probs_T, v_part, first in ((pT_all, v_sb[:, slot, :], True), (pT_prev, v_change[:, a, :], False)):
                    for hh in range(4):
                        head = grp * 4 + hh
                        ins = mm(o_ps[32 * hh:32 * hh + 32, grp * P:(grp + 1) * P], v_part[:, head * DH:(head + 1) * DH],
                                 probs_T[:, s % 2, hh * P:(hh + 1) * P], start=first, stop=not first, tile_position=(0, 32 * hh))
                ins.then_inc(pv_done, 1)

            def probs_transposed(i, h, s):
                step = (i * 2 + h) * 8 + s
                wait(pe, probs_scaled, step + 1)
                wait(pe, pT_copied, step)
                for hh in range(4):
                    ins = nc.tensor.transpose(pT_ps[:, hh * P:(hh + 1) * P], probs[:, s % 2, hh * P:(hh + 1) * P], ident[:, :])
                ins.then_inc(pT_done, 1)

            held = [None, None]

            def run_units(units, pair, h, i):
                for u, unit in units:
                    if not unit_exists(unit, i, h):
                        continue
                    if held[u % 2] is not None:
                        wait(pe, *held[u % 2])
                    run_unit(unit, u, pair, h)
                    held[u % 2] = (CONSUMED[unit[0]], unit_index(unit, pair) + 1)

            body_of[0] = -1
            for u, (unit, pair) in enumerate(PROJECTION):
                run_units([(u, unit)], pair, pair % 2, -1)
            pe.wait_ge(init3, 2)
            scores(0, 0, 0)
            scores(0, 0, 1)

            def body(i):
                body_of[0] = i
                if not is_first(i):
                    for u in (16, 17):
                        held[u % 2] = (CONSUMED[UNITS[u][0]], unit_index(UNITS[u], i * 2 - 1) + 1)
                for h in range(2):
                    pair, u = i * 2 + h, 0
                    for s in range(8):
                        ahead = AHEAD[s]
                        units = list(enumerate(SCHEDULE[s], u))
                        if not (is_last(i, NB) and h == 1 and s >= 6):
                            scores(i, h, s + 2)
                        run_units(units[:ahead], pair, h, i)
                        values(i, h, s - 1)
                        probs_transposed(i, h, s)
                        run_units(units[ahead:], pair, h, i)
                        u += len(SCHEDULE[s])

            repeated(pe, NB, body)
            values(NB - 1, 1, 7)
            for unit in (("wo", 1, 0), ("wo", 1, 1)):
                u = unit[2]
                wait(pe, *held[u % 2])
                run_unit(unit, u, NP, 0)
                held[u % 2] = (CONSUMED[unit[0]], unit_index(unit, NP) + 1)

        @block.scalar
        def _(act):
            sc = nc.scalar

            def roots(i):
                for r in range(2):
                    wait(act, root_wanted, i * 2 + r + 1)
                    sc.activation(root[:, :], ve[:, :], ACT.Sqrt).then_inc(root_made, 1)

            def norms(i, js):
                for j in js:
                    n = i * TB + j
                    wait(act, xa_out[j], i * 16)
                    wait(act, t_done, n + 1 - TB)
                    sc.activation(xa1[:, j, :], x1[:, j, :], ACT.Identity, bias=nbias[:, j:j + 1], scale=comb[:, j:j + 1]).then_inc(xa_made, 1)

            def front(i):
                for j in range(TB):
                    n = i * TB + j
                    wait(act, t_done, n + 1)
                    wait(act, logits_done, n - 1)
                    sc.activation(xT1[:, j % 2, :, :], t_ps[j % 2][:, :], ACT.Copy).then_inc(xT_made, 1)
                    if j + 2 < TB:
                        norms(i, range(j + 2, j + 3))
                    if j:
                        keep(i, j - 1)
                keep(i, TB - 1)

            def keep(i, j):
                n = i * TB + j
                wait(act, logits_done, n + 1)
                sc.activation(logit_all[:, bass.ds(n, 1), :], logit_ps[j % 2][:, 0:E], ACT.Copy)
                wait(act, logits_ranked, n + 1 - TB)
                sc.activation(logit_now[:, j, :], logit_ps[j % 2][:, 0:E], ACT.Copy).then_inc(logits_kept, 1)

            def tiles(i):
                roots(i)
                wait(act, factors_made, i + 1)
                norms(i, range(2))
                front(i)

            tiles(0)

            def norm_body(i):
                if not is_last(i, NB):
                    tiles(i + 1)

            repeated(act, NB, norm_body)

            act.wait_ge(nmax_made, 2)
            act.wait_ge(logits_kept, NT)

            def sums(i):
                for j in range(TB):
                    n = i * TB + j
                    if j >= 2:
                        wait(act, z_made, n - 1)
                    elif not is_first(i):
                        wait(act, z_made, n - 1)
                    sc.activation(junk_z[:, j % 2, :], logit_all[:, bass.ds(n, 1), :], ACT.Exp, bias=nmax[:, bass.ds(n, 1)],
                                  scale=ir2[:, bass.ds(n, 1)], accum_out=zsum[:, bass.ds(n, 1)]).then_inc(z_made, 1)

            repeated(act, NB, sums)
            sc.activation(gb[:, :], ga[:, :], ACT.Exp).then_inc(gate_exp, 1)

            def expert_body(i):
                for b in range(EB):
                    n = i * EB + b
                    wait(act, y_done, n + 1)
                    wait(act, ysb_out[b], i * 16)
                    sc.activation(ysb[:, b, :], y_ps[b % 2][:, :], ACT.Copy).then_inc(y_copied, 1)
                    wait(act, y_copied, n + 1)
                    act.dma_start(yb_rows[bass.ds(n * P, P), :], ysb[:, b, :]).then_inc(ysb_out[b], 16)

            repeated(act, NE, expert_body)

            experts_done(act)

            def half(u):
                return unit_ps[u % 2][:, 0:256]

            def read_unit(unit, u, pair):
                kind, a, c = unit
                idx = unit_index(unit, pair)
                if kind == "xT":
                    wait(act, xT_tr, idx + 1)
                    sc.activation(xT_hi[:, :, a * P:(a + 1) * P], unit_ps[u % 2][:, :], ACT.Copy).then_inc(xT_hi_made, 1)
                elif kind == "kq":
                    wait(act, kq_done, idx + 1)
                    if c == 0:
                        wait(act, (k_stacked, q_stacked)[a], (pair + 1) * STACK_DMAS * 16)
                    sc.activation(kq_hi[:, a, c, :], half(u), ACT.Copy).then_inc(kq_hi_made, 1)
                elif kind == "v":
                    wait(act, v_done, idx + 1)
                    slot = v_slot(pair, a)
                    wait(act, v_changed, pair * 2 + 2 + a - 2)
                    sc.activation(v_sb[:, slot, c * 256:(c + 1) * 256], half(u), ACT.Copy).then_inc(v_made, 1)

            def copy_pT(i, h, s):
                step = (i * 2 + h) * 8 + s
                wait(act, pT_done, step + 1)
                wait(act, pv_done, step - 1)
                sc.activation(pT_all[:, s % 2, :], pT_ps[:, :], ACT.Copy).then_inc(pT_copied, 1)

            def read_o(n):
                wait(act, pv_done, n * 4 + 4)
                wait(act, h_done, n * 2)
                sc.activation(oT_hi[:, :, :], o_ps[:, :], ACT.Copy).then_inc(oT_hi_made, 1)

            h_now = [0]

            def v_slot(pair, a):
                return 2 * (1 - h_now[0]) + a

            def exps(i, h, s):
                if s >= 8:
                    i, h, s = (i, 1, s - 8) if h == 0 else (i + 1, 0, s - 8)
                step = (i * 2 + h) * 8 + s
                wait(act, nmx_made, step + 1)
                wait(act, pT_done, step - 1)
                for hh in range(4):
                    ins = sc.activation(probs[:, s % 2, hh * P:(hh + 1) * P], score_ps[s % 2][1][:, hh * P:(hh + 1) * P], ACT.Exp,
                                        bias=nmx[:, s % 2, hh:hh + 1], scale=SCALE,
                                        accum_out=psum_row[:, s % 2, hh:hh + 1])
                ins.then_inc(probs_made, 1)

            h_now[0] = 1
            for u, (unit, pair) in enumerate(PROJECTION):
                read_unit(unit, u, pair)
            exps(0, 0, 0)
            exps(0, 0, 1)

            def body(i):
                for h in range(2):
                    h_now[0] = h
                    pair, u = i * 2 + h, 0
                    for s in range(8):
                        ahead = AHEAD[s]
                        for unit in SCHEDULE[s][:ahead]:
                            if unit_exists(unit, i, h):
                                read_unit(unit, u, pair)
                            u += 1
                        if s == 0 and not (is_first(i) and h == 0):
                            read_o(pair * 2 - 1)
                        if s == 4:
                            read_o(pair * 2)
                        copy_pT(i, h, s)
                        for unit in SCHEDULE[s][ahead:ahead + READ_EARLY[s]]:
                            if unit_exists(unit, i, h):
                                read_unit(unit, u, pair)
                            u += 1
                        if not (is_last(i, NB) and h == 1 and s >= 6):
                            exps(i, h, s + 2)
                        for unit in SCHEDULE[s][ahead + READ_EARLY[s]:]:
                            if unit_exists(unit, i, h):
                                read_unit(unit, u, pair)
                            u += 1

            repeated(act, NB, body)
            read_o(NT - 1)

        @block.vector
        def _(dve):
            ve_ = nc.vector
            STATS, ROUTE = 22, 24

            def newton(chain, y, v):
                chain.settle()
                chain.did(ve_.scalar_tensor_tensor(tmp4[:, :], y[:, :], -0.5, y[:, :], ALU.mult, ALU.mult))
                chain.settle()
                chain.did(ve_.tensor_tensor(tmp4[:, :], tmp4[:, :], v[:, :], ALU.mult))
                chain.settle()
                chain.did(ve_.scalar_tensor_tensor(y[:, :], tmp4[:, :], 1.5, y[:, :], ALU.add, ALU.mult))

            def stats(i):
                chain = Chain(dve, stat_step, i * STATS)
                for j in range(TB):
                    wait(dve, x_in[j], i * 16 + 16)
                    chain.did(ve_.bn_stats(bn6[:, j, :], x1[:, j, :]))
                chain.settle()
                for j in range(TB):
                    chain.did(apart(ve_.bn_aggr(mv[:, j, :], bn6[:, j, :])))
                chain.settle()
                ve_.tensor_scalar(ve[:, :], mv[:, :, 1], LN_EPS, None, ALU.add).then_inc(root_wanted, 1)
                wait(dve, root_made, i * 2 + 1)
                chain.did(ve_.reciprocal(rstd[:, :], root[:, :]))
                newton(chain, rstd, ve)
                chain.settle()
                chain.did(ve_.tensor_tensor(ms[:, :], rstd[:, :], rstd[:, :], ALU.mult))
                chain.settle()
                chain.did(ve_.tensor_tensor(ms[:, :], ms[:, :], mv[:, :, 1], ALU.mult))
                chain.settle()
                ve_.tensor_scalar(ve[:, :], ms[:, :], RMS_EPS, None, ALU.add).then_inc(root_wanted, 1)
                wait(dve, root_made, i * 2 + 2)
                chain.did(ve_.reciprocal(r2[:, :], root[:, :]))
                newton(chain, r2, ve)
                chain.settle()
                wait(dve, xa_made, i * TB)
                wait(dve, xpx_made, i * TB)
                chain.did(ve_.tensor_tensor(comb[:, :], rstd[:, :], r2[:, :], ALU.mult))
                chain.did(ve_.tensor_tensor(ir2[:, bass.ds(i * TB, TB)], ve[:, :], r2[:, :], ALU.mult))
                chain.did(ve_.tensor_scalar(rplus[:, :], rstd[:, :], 1.0, None, ALU.add))
                chain.did(ve_.scalar_tensor_tensor(nbias_x[:, :], mv[:, :, 0], -1.0, rstd[:, :], ALU.mult, ALU.mult))
                chain.settle()
                ve_.scalar_tensor_tensor(nbias[:, :], mv[:, :, 0], -1.0, comb[:, :], ALU.mult, ALU.mult).then_inc(factors_made, 1)
                wait(dve, factors_made, i + 1)
                assert chain.n == STATS, chain.n

            def route(i):
                chain = Chain(dve, route_step, i * ROUTE)
                now = bass.ds(i * TB, TB)
                for j in range(TB):
                    wait(dve, logits_kept, i * TB + j + 1)
                    chain.did(apart(ve_.max(top8[:, j, :], logit_now[:, j, :])))
                chain.settle()
                for j in range(TB):
                    apart(ve_.max_index(idx8[:, j, :], top8[:, j, :], logit_now[:, j, :])).then_inc(logits_ranked, 1)
                wait(dve, logits_ranked, (i + 1) * TB)
                for c, (keep_e, keep_l) in enumerate(((e1, l1), (e2, l2))):
                    chain.did(ve_.tensor_copy(e12[:, c, :], idx8[:, :, c]))
                    chain.did(ve_.tensor_copy(keep_e[:, now], idx8[:, :, c]))
                    chain.did(ve_.tensor_copy(keep_l[:, now], top8[:, :, c]))
                chain.settle()
                for j in range(TB):
                    n = i * TB + j
                    wait(dve, table_done, n + 1 - TB)
                    wait(dve, mask2_kept, n + 1 - TB)
                    for c in range(2):
                        chain.did(ve_.tensor_scalar(mask[:, j, c * E:(c + 1) * E], iota_row[:, :], e12[:, c, j:j + 1], None, ALU.is_equal))
                    if j == TB - 1:
                        wait(dve, mask_made, i * TB + j)
                        wait(dve, pos_done, i * TB + 1)
                    chain.settle()
                    if j:
                        wait(dve, mask_made, n)
                    elif not is_first(i):
                        wait(dve, mask_made, i * TB)
                    ve_.tensor_tensor(before[:, (j + 1) % TB, :], before[:, j, :], mask[:, j, :], ALU.add).then_inc(mask_made, 1)
                for j in range(TB):
                    n = i * TB + j
                    wait(dve, pos_done, n + 1)
                    chain.did(ve_.scalar_tensor_tensor(junk[:, j, :], pos_ps[j % 2][:, 0:E], 1.0, mask[:, j, 0:E], ALU.mult, ALU.mult,
                                                       accum_out=loc4[:, 0, j:j + 1]))
                    ve_.scalar_tensor_tensor(junk2[:, j, :], pos_ps[j % 2][:, E:2 * E], 1.0, mask[:, j, E:2 * E], ALU.mult, ALU.mult,
                                             accum_out=loc4[:, 1, j:j + 1]).then_inc(pos_read, 1)
                wait(dve, pos_read, (i + 1) * TB)
                chain.settle()
                for j in range(TB):
                    n = i * TB + j
                    ve_.scalar_tensor_tensor(place[:, j, :].rearrange("p (a c) -> p a c", a=2), iota_row[:, :].unsqueeze(1).to_broadcast([P, 2, CAP]),
                                             loc4[:, 0, j:j + 1], lane_tile[:, bass.ds(n, 1), :].rearrange("p a b -> p (a b)").unsqueeze(2).to_broadcast([P, 2, CAP]),
                                             ALU.is_equal, ALU.mult).then_inc(place_made, 1)
                chain.did(ve_.tensor_copy(loc1[:, now], loc4[:, 0, :]))
                chain.did(ve_.tensor_copy(rank2[:, now], loc4[:, 1, :]))
                wait(dve, place_made, (i + 1) * TB)
                chain.settle()
                assert chain.n == ROUTE, chain.n

            dve.wait_ge(const_made, CONSTS + 4 + B)
            stats(0)

            def norm_body(i):
                if not is_last(i, NB):
                    stats(i + 1)
                route(i)

            repeated(dve, NB, norm_body)

            dve.wait_ge(count_done, 1)
            late = Chain(dve, late_step, 0)
            late.did(ve_.tensor_copy(count1[:, :], pos_ps[0][:, 0:E]))
            late.did(ve_.tensor_tensor(gc[:, :], l2[:, :], l1[:, :], ALU.subtract))
            ve_.scalar_tensor_tensor(nmax[:, :], l1[:, :], -1.0, ir2[:, :], ALU.mult, ALU.mult).then_inc(nmax_made, 1)
            late.settle()
            ve_.tensor_tensor(ga[:, :], gc[:, :], ir2[:, :], ALU.mult).then_inc(nmax_made, 1)

            def second_bases(i):
                for j in range(TB):
                    n = i * TB + j
                    wait(dve, base_step, n + 1 - TB)
                    ve_.scalar_tensor_tensor(junk[:, j, :], iota_row[:, :], e2[:, bass.ds(n, 1)], count1[:, :],
                                             ALU.is_equal, ALU.mult, accum_out=base2[:, bass.ds(n, 1)]).then_inc(base_step, 1)

            repeated(dve, NB, second_bases)
            dve.wait_ge(base_step, NT)
            late.did(ve_.tensor_tensor(loc2[:, :], base2[:, :], rank2[:, :], ALU.add))
            late.settle()
            dve.wait_ge(table_done, NT)

            def second_places(i):
                for j in range(TB):
                    n = i * TB + j
                    wait(dve, table2_done, n + 1 - TB)
                    ve_.scalar_tensor_tensor(place[:, j, :].rearrange("p (a c) -> p a c", a=2), iota_row[:, :].unsqueeze(1).to_broadcast([P, 2, CAP]),
                                             loc2[:, bass.ds(n, 1)], lane_tile[:, bass.ds(n, 1), :].rearrange("p a b -> p (a b)").unsqueeze(2).to_broadcast([P, 2, CAP]),
                                             ALU.is_equal, ALU.mult).then_inc(place2_made, 1)

            repeated(dve, NB, second_places)
            dve.wait_ge(table2_done, NT)
            late.did(ve_.tensor_scalar(ids_hi[:, :], table_ps[:, CAP:2 * CAP], float(P), None, ALU.mult))
            late.settle()
            ve_.tensor_tensor(ids[:, :], table_ps[:, 0:CAP], ids_hi[:, :], ALU.add).then_inc(ids_made, 1)
            dve.wait_ge(idsT_done, 1)
            ve_.tensor_copy(idx_all[:, :], pos_ps[1][:, 0:P]).then_inc(idx_made, 1)

            def expert_body(i):
                for b in range(EB):
                    n = i * EB + b
                    wait(dve, rowsT_done, n + 1)
                    wait(dve, y_done, n - 1)
                    ve_.tensor_copy(rowsT[:, b % 2, :, :], t_ps[b % 2][:, :].rearrange("p (k c) -> p k c", k=KT)).then_inc(rowsT_made, 1)

            repeated(dve, NE, expert_body)

            dve.wait_ge(z_made, NT)
            dve.wait_ge(gate_exp, 1)

            def step(ins):
                late.did(ins)
                late.settle()

            step(ve_.reciprocal(ga[:, :], zsum[:, :]))
            step(ve_.tensor_tensor(gb[:, :], gb[:, :], ga[:, :], ALU.mult))
            step(ve_.tensor_tensor(gc[:, :], ga[:, :], gb[:, :], ALU.add))
            step(ve_.tensor_scalar(gc[:, :], gc[:, :], GATE_EPS, None, ALU.max))
            step(ve_.reciprocal(zsum[:, :], gc[:, :]))
            step(ve_.tensor_tensor(zsum[:, :], zsum[:, :], ir2[:, :], ALU.mult))
            for gate, e, loc, weight, slot in ((ga, e1, loc1, w1, slot1), (gb, e2, loc2, w2, slot2)):
                step(ve_.tensor_tensor(gate[:, :], gate[:, :], zsum[:, :], ALU.mult))
                step(ve_.tensor_scalar(gc[:, :], loc[:, :], float(CAP), None, ALU.is_lt))
                step(ve_.tensor_tensor(weight[:, :], gate[:, :], gc[:, :], ALU.mult))
                step(ve_.tensor_scalar(gc[:, :], loc[:, :], float(CAP - 1), None, ALU.min))
                step(ve_.scalar_tensor_tensor(gate[:, :], e[:, :], float(CAP), gc[:, :], ALU.mult, ALU.add))
                step(ve_.tensor_copy(slot[:, :], gate[:, :]))
            ve_.memset(tmp4[:, :], 0.0).then_inc(routing_made, 1)

            experts_done(dve)

            def half(u):
                return unit_ps[u % 2][:, 0:256]

            def read_unit(unit, u, pair):
                kind, a, c = unit
                idx = unit_index(unit, pair)
                if kind == "xT":
                    wait(dve, xT_hi_made, idx + 1)
                    cols = slice(a * P, (a + 1) * P)
                    ve_.tensor_tensor(xT_lo[:, :, cols], unit_ps[u % 2][:, :].rearrange("p (k c) -> p k c", k=KT),
                                      xT_hi[:, :, cols].bitcast(F32), ALU.subtract).then_inc(xT_split, 1)
                elif kind == "kq":
                    wait(dve, kq_hi_made, idx + 1)
                    ve_.tensor_tensor(kq_lo[:, a, c, :], half(u), kq_hi[:, a, c, :].bitcast(F32), ALU.subtract).then_inc(kq_split, 1)
                elif kind == "wo":
                    wait(dve, h_done, idx + 1)
                    slot = (2 * h_now[0] + (0 if a == 0 else -1)) % 4
                    cols = slice(c * 256, (c + 1) * 256)
                    ve_.tensor_tensor(acc[:, slot, cols], half(u), acc[:, slot, cols], ALU.add).then_inc(fin_done, 1)

            h_now = [0]
            MERGE = 2 * 16 + 4

            def merge(i, h, s, chain):
                if s >= 8:
                    i, h, s = (i, 1, s - 8) if h == 0 else (i + 1, 0, s - 8)
                step, a = (i * 2 + h) * 8 + s, s // 4
                prev, cur = score_ps[s % 2]
                wait(dve, score_done, step + 1)
                if h == 0 and a == 0:
                    chain.did(ve_.tensor_scalar(prev[:, :], prev[:, :], prev_cap[:, bass.ds(i, 1)], None, ALU.min))
                    chain.settle()
                chain.did(apart(ve_.copy_predicated(cur[:, :], above[:, :, :], prev[:, :])))
                chain.settle()
                wait(dve, probs_made, step - 1)
                chain.did(ve_.tensor_reduce(mx[:, s % 2, :], cur[:, :].rearrange("p (h c) -> p h c", h=4), AX.X, ALU.max))
                chain.settle()
                ve_.tensor_scalar(nmx[:, s % 2, :], mx[:, s % 2, :], -SCALE, None, ALU.mult).then_inc(nmx_made, 1)

            def invert_sums(i, h, s):
                if s == 8:
                    i, h, s = (i, 1, 0) if h == 0 else (i + 1, 0, 0)
                step = (i * 2 + h) * 8 + s
                wait(dve, probs_made, step + 1)
                wait(dve, probs_scaled, step - 1)
                ve_.reciprocal(rsum[:, s % 2, :], psum_row[:, s % 2, :]).then_inc(rsum_made, 1)

            def split_o(n):
                wait(dve, oT_hi_made, n + 1)
                ve_.tensor_tensor(oT_lo[:, :, :], o_ps[:, :].rearrange("p (k c) -> p k c", k=KT), oT_hi[:, :, :].bitcast(F32),
                                  ALU.subtract).then_inc(oT_split, 1)

            def combine(n, a, slot, i):
                k = i
                wait(dve, acc_in[slot], k * 16 + 16)
                rounds = k * 2 + (slot // 2) + 1
                wait(dve, y1_in[a], rounds * 16)
                wait(dve, y2_in[a], rounds * 16)
                ve_.scalar_tensor_tensor(acc[:, slot, :], y1[:, a, :], w1[:, bass.ds(n, 1)], acc[:, slot, :], ALU.mult, ALU.add).then_inc(comb_step, 1)
                wait(dve, comb_step, n * 2 + 1)
                ve_.scalar_tensor_tensor(acc[:, slot, :], y2[:, a, :], w2[:, bass.ds(n, 1)], acc[:, slot, :], ALU.mult, ALU.add).then_inc(comb_step, 1)

            for u, (unit, pair) in enumerate(PROJECTION):
                read_unit(unit, u, pair)
            chain = Chain(dve, merge_step, 0)
            merge(0, 0, 0, chain)
            merge(0, 0, 1, chain)
            invert_sums(0, 0, 0)
            FIRST = chain.n

            def body(i):
                chain = Chain(dve, merge_step, i * MERGE + FIRST)
                for h in range(2):
                    h_now[0] = h
                    pair, u = i * 2 + h, 0
                    for s in range(8):
                        ahead = AHEAD[s]
                        if not (is_last(i, NB) and h == 1 and s == 7):
                            invert_sums(i, h, s + 1)
                        if not (is_last(i, NB) and h == 1 and s >= 6):
                            merge(i, h, s + 2, chain)
                        for unit in SCHEDULE[s][:ahead]:
                            if unit_exists(unit, i, h):
                                if unit[0] == "wo":
                                    wait(dve, comb_step, (pair * 2 - (1 if unit[1] else 0)) * 2 + 2)
                                read_unit(unit, u, pair)
                            u += 1
                        if s == 0 and not (is_first(i) and h == 0):
                            split_o(pair * 2 - 1)
                        if s == 4:
                            split_o(pair * 2)
                        if s == 4:
                            combine(pair * 2, 0, 2 * h, i)
                        if s == 6:
                            combine(pair * 2 + 1, 1, 2 * h + 1, i)
                        for unit in SCHEDULE[s][ahead:]:
                            if unit_exists(unit, i, h):
                                if unit[0] == "wo":
                                    wait(dve, comb_step, (pair * 2 - (1 if unit[1] else 0)) * 2 + 2)
                                read_unit(unit, u, pair)
                            u += 1
                if not is_last(i, NB):
                    assert chain.n == MERGE, chain.n

            repeated(dve, NB, body)
            h_now[0] = 0
            split_o(NT - 1)
            for unit in (("wo", 1, 0), ("wo", 1, 1)):
                wait(dve, comb_step, NT * 2)
                read_unit(unit, unit[2], NP)


_INS = ["L0_attn_x", "L0_attn_g", "L0_attn_Wqkv", "L0_attn_Wo", "L0_ffn_wg", "L0_ffn_we"]


def kernel(**inputs):
    import numpy as np
    from concourse import bacc
    from concourse.bass_utils import run_bass_kernel_spmd

    nc = bacc.Bacc("TRN2", target_bir_lowering=False, num_devices=1)
    arrays, args = {}, []
    for name in _INS:
        a = np.ascontiguousarray(inputs[name])
        arrays[f"in_{name}"] = a
        args.append(nc.dram_tensor(f"in_{name}", a.shape, mybir.dt.from_np(a.dtype), kind="ExternalInput").ap())
    out = nc.dram_tensor("out", arrays["in_L0_attn_x"].shape, F32, kind="ExternalOutput").ap()
    telephone_moe(nc, *args, out)
    r = run_bass_kernel_spmd(nc, [arrays], core_ids=[0])
    return r.results[0]["out"]
```
